# Optimizing a Trainium2 kernel written in Bass

```python
import numpy as np
import jax
import jax.numpy as jnp

def _softmax(x, axis=-1):
    return jax.nn.softmax(x, axis=axis)

def _gelu(x):
    return jax.nn.gelu(x, approximate=True)

def _silu(x):
    return jax.nn.silu(x)

def _sigmoid(x):
    return jax.nn.sigmoid(x)

def _layernorm(x, axis=-1, eps=1e-05):
    m = jnp.mean(x, axis=axis, keepdims=True)
    v = jnp.var(x, axis=axis, keepdims=True)
    return (x - m) / jnp.sqrt(v + eps)

def _scatter_add(tgt, idx, src, axis=0):
    return tgt.at[idx].add(src)

def _segment_sum(src, seg, n):
    return jax.ops.segment_sum(src, seg, n)
kernel_name = 'mk_seq_preln_d2_jaxref_r8_df241a'

def setup_inputs(seed: int=0):
    np.random.seed(seed)
    _w = jnp.asarray

    def _L0_attn_setup():
        import jax, jax.numpy as jnp
        import numpy as np
        D = 128
        H = 16
        DK = D // H
        SCALE = 1.0 / np.sqrt(DK).astype(np.float32)
        key = jax.random.key(seed)
        ks = jax.random.split(key, 9)
        N, S = (4, 256)
        w = 0.02
        return {'x': jax.random.normal(ks[0], (N, S, D), dtype=jnp.float32), 'Wq': jax.random.normal(ks[1], (D, D), dtype=jnp.float32) * w, 'bq': jnp.zeros((D,), dtype=jnp.float32), 'Wk': jax.random.normal(ks[2], (D, D), dtype=jnp.float32) * w, 'bk': jnp.zeros((D,), dtype=jnp.float32), 'Wv': jax.random.normal(ks[3], (D, D), dtype=jnp.float32) * w, 'bv': jnp.zeros((D,), dtype=jnp.float32), 'Wp': jax.random.normal(ks[4], (D, D), dtype=jnp.float32) * w, 'bp': jnp.zeros((D,), dtype=jnp.float32)}
    _L0_attn_in = _L0_attn_setup()

    def _L0_ffn_setup():
        import jax, jax.numpy as jnp
        import numpy as np
        R = 64
        key = jax.random.key(seed)
        k1, k2, k3 = jax.random.split(key, 3)
        B, S, D_IN, D_OUT = (8, 512, 128, 128)
        x = jax.random.normal(k1, (B, S, D_IN), dtype=jnp.float32)
        weight = jax.random.normal(k2, (D_OUT, D_IN), dtype=jnp.float32) * (1.0 / np.sqrt(D_IN))
        disha = jax.random.normal(k3, (R, D_OUT), dtype=jnp.float32) * 0.01
        return {'x': x, 'weight': weight, 'disha': disha}
    _L0_ffn_in = _L0_ffn_setup()

    def _L1_attn_setup():
        import jax, jax.numpy as jnp
        import numpy as np
        EMBED_DIM = 128
        HEADS = 16
        HEAD_DIM = EMBED_DIM // HEADS
        key = jax.random.key(seed)
        ks = jax.random.split(key, 9)
        B, T, C = (4, 512, EMBED_DIM)
        s = 1.0 / np.sqrt(C)
        inp = {'x': jax.random.normal(ks[0], (B, T, C), dtype=jnp.float32), 'Wq': jax.random.normal(ks[1], (C, C), dtype=jnp.float32) * s, 'bq': jnp.zeros((C,), dtype=jnp.float32), 'Wk': jax.random.normal(ks[2], (C, C), dtype=jnp.float32) * s, 'bk': jnp.zeros((C,), dtype=jnp.float32), 'Wv': jax.random.normal(ks[3], (C, C), dtype=jnp.float32) * s, 'bv': jnp.zeros((C,), dtype=jnp.float32), 'Wc': jax.random.normal(ks[4], (C, C), dtype=jnp.float32) * s, 'bc': jnp.zeros((C,), dtype=jnp.float32)}
        return inp
    _L1_attn_in = _L1_attn_setup()

    def _L1_ffn_setup():
        import jax, jax.numpy as jnp
        import numpy as np

        def _bitlinear(x, w_latent):
            scale = jax.lax.stop_gradient(jnp.clip(jnp.mean(jnp.abs(w_latent), axis=1, keepdims=True), 1e-05, None))
            tern = jnp.clip(jnp.round(w_latent / scale), -1.0, 1.0)
            w = w_latent + jax.lax.stop_gradient(tern - w_latent)
            return x @ (w * scale).T
        key = jax.random.key(seed)
        ks = jax.random.split(key, 6)
        dim, hidden, rank = (128, 512, 16)
        B, S = (4, 512)
        x = jax.random.normal(ks[0], (B, S, dim), dtype=jnp.float32)
        w_fc = 0.02 * jax.random.normal(ks[1], (hidden, dim), dtype=jnp.float32)
        w_proj = 0.02 * jax.random.normal(ks[2], (dim, hidden), dtype=jnp.float32)
        u = 0.02 * jax.random.normal(ks[3], (hidden, rank), dtype=jnp.float32)
        v = 0.02 * jax.random.normal(ks[4], (rank, dim), dtype=jnp.float32)
        fast_b = jax.random.normal(ks[5], (rank, rank), dtype=jnp.float32)
        gate = jnp.float32(0.05)
        return {'x': x, 'fast_b': fast_b, 'w_fc': w_fc, 'w_proj': w_proj, 'u': u, 'v': v, 'gate': gate}
    _L1_ffn_in = _L1_ffn_setup()
    _d = {'L0_attn_x': _L0_attn_in['x'], 'L0_attn_Wq': _L0_attn_in['Wq'], 'L0_attn_bq': _L0_attn_in['bq'], 'L0_attn_Wk': _L0_attn_in['Wk'], 'L0_attn_bk': _L0_attn_in['bk'], 'L0_attn_Wv': _L0_attn_in['Wv'], 'L0_attn_bv': _L0_attn_in['bv'], 'L0_attn_Wp': _L0_attn_in['Wp'], 'L0_attn_bp': _L0_attn_in['bp'], 'L0_ffn_weight': _L0_ffn_in['weight'], 'L0_ffn_disha': _L0_ffn_in['disha'], 'L1_attn_Wq': _L1_attn_in['Wq'], 'L1_attn_bq': _L1_attn_in['bq'], 'L1_attn_Wk': _L1_attn_in['Wk'], 'L1_attn_bk': _L1_attn_in['bk'], 'L1_attn_Wv': _L1_attn_in['Wv'], 'L1_attn_bv': _L1_attn_in['bv'], 'L1_attn_Wc': _L1_attn_in['Wc'], 'L1_attn_bc': _L1_attn_in['bc'], 'L1_ffn_fast_b': _L1_ffn_in['fast_b'], 'L1_ffn_w_fc': _L1_ffn_in['w_fc'], 'L1_ffn_w_proj': _L1_ffn_in['w_proj'], 'L1_ffn_u': _L1_ffn_in['u'], 'L1_ffn_v': _L1_ffn_in['v'], 'L1_ffn_gate': _L1_ffn_in['gate']}
    _x0 = _d['L0_attn_x']
    _d['L0_attn_x'] = jax.random.normal(jax.random.fold_in(jax.random.key(seed), 1), (16, 256, 128), dtype=_x0.dtype)
    del _x0
    return _d

def reference(L0_attn_x, L0_attn_Wq, L0_attn_bq, L0_attn_Wk, L0_attn_bk, L0_attn_Wv, L0_attn_bv, L0_attn_Wp, L0_attn_bp, L0_ffn_weight, L0_ffn_disha, L1_attn_Wq, L1_attn_bq, L1_attn_Wk, L1_attn_bk, L1_attn_Wv, L1_attn_bv, L1_attn_Wc, L1_attn_bc, L1_ffn_fast_b, L1_ffn_w_fc, L1_ffn_w_proj, L1_ffn_u, L1_ffn_v, L1_ffn_gate):

    def _L0_attn_ref(x, Wq, bq, Wk, bk, Wv, bv, Wp, bp):
        import jax, jax.numpy as jnp
        import numpy as np
        D = 128
        H = 16
        DK = D // H
        SCALE = 1.0 / np.sqrt(DK).astype(np.float32)
        N, S, _ = x.shape

        def heads(W, b):
            h = jnp.einsum('nsd,ed->nse', x, W) + b
            return h.reshape(N, S, H, DK).transpose(0, 2, 1, 3)
        q = heads(Wq, bq)
        k = heads(Wk, bk)
        v = heads(Wv, bv)
        att = jnp.einsum('nhsd,nhtd->nhst', q, k) * SCALE
        att = jax.nn.softmax(att, axis=-1)
        y = jnp.einsum('nhst,nhtd->nhsd', att, v)
        y = y.transpose(0, 2, 1, 3).reshape(N, S, D)
        return jnp.einsum('nsd,ed->nse', y, Wp) + bp

    def _L0_ffn_ref(x, weight, disha):
        import jax, jax.numpy as jnp
        import numpy as np
        R = 64
        result = jnp.einsum('bsd,od->bso', x, weight)
        r = disha.shape[0]
        pooled = x.reshape(*x.shape[:-1], x.shape[-1] // r, r).sum(axis=-2)
        return result + pooled @ disha

    def _L1_attn_ref(x, Wq, bq, Wk, bk, Wv, bv, Wc, bc):
        import jax, jax.numpy as jnp
        import numpy as np
        EMBED_DIM = 128
        HEADS = 16
        HEAD_DIM = EMBED_DIM // HEADS
        B, T, C = x.shape
        H, D = (HEADS, HEAD_DIM)
        q = (x @ Wq.T + bq).reshape(B, T, H, D).transpose(0, 2, 1, 3)
        k = (x @ Wk.T + bk).reshape(B, T, H, D).transpose(0, 2, 1, 3)
        v = (x @ Wv.T + bv).reshape(B, T, H, D).transpose(0, 2, 1, 3)
        q = jax.nn.elu(q) + 1.0
        k = jax.nn.elu(k) + 1.0
        kv = jnp.einsum('bhtd,bhte->bhde', k, v)
        k_sum = k.sum(axis=2)
        z = 1.0 / (jnp.einsum('bhtd,bhd->bht', q, k_sum)[..., None] + 1e-06)
        y = jnp.einsum('bhtd,bhde->bhte', q, kv) * z
        y = y.transpose(0, 2, 1, 3).reshape(B, T, C)
        return y @ Wc.T + bc

    def _L1_ffn_ref(x, fast_b, w_fc, w_proj, u, v, gate):
        import jax, jax.numpy as jnp
        import numpy as np

        def _bitlinear(x, w_latent):
            scale = jax.lax.stop_gradient(jnp.clip(jnp.mean(jnp.abs(w_latent), axis=1, keepdims=True), 1e-05, None))
            tern = jnp.clip(jnp.round(w_latent / scale), -1.0, 1.0)
            w = w_latent + jax.lax.stop_gradient(tern - w_latent)
            return x @ (w * scale).T
        h = _bitlinear(x, w_fc) + gate * (x @ v.T @ fast_b.T @ u.T)
        r = jnp.maximum(h, 0.0)
        return _bitlinear(r * r, w_proj)
    x = L0_attn_x
    x = x + _L0_attn_ref(_layernorm(x, axis=-1), L0_attn_Wq, L0_attn_bq, L0_attn_Wk, L0_attn_bk, L0_attn_Wv, L0_attn_bv, L0_attn_Wp, L0_attn_bp)
    x = x + _L0_ffn_ref(_layernorm(x, axis=-1), L0_ffn_weight, L0_ffn_disha)
    x = x + _L1_attn_ref(_layernorm(x, axis=-1), L1_attn_Wq, L1_attn_bq, L1_attn_Wk, L1_attn_bk, L1_attn_Wv, L1_attn_bv, L1_attn_Wc, L1_attn_bc)
    x = x + _L1_ffn_ref(_layernorm(x, axis=-1), L1_ffn_fast_b, L1_ffn_w_fc, L1_ffn_w_proj, L1_ffn_u, L1_ffn_v, L1_ffn_gate)
    return x

_drawn_inputs = setup_inputs


def setup_inputs(seed=0):
    import zlib

    import numpy as np

    out = dict(_drawn_inputs(seed))
    spreads = {'L0_attn_bq': (0.0, 0.8),
     'L0_attn_bk': (0.0, 0.8),
     'L0_attn_bv': (0.0, 0.315),
     'L0_attn_bp': (0.0, 0.1),
     'L1_attn_bq': (0.0, 0.8),
     'L1_attn_bk': (0.0, 0.8),
     'L1_attn_bv': (0.0, 0.1),
     'L1_attn_bc': (0.0, 0.1)}
    factors = {'L0_attn_Wq': 8.0,
     'L0_attn_Wk': 8.0,
     'L0_attn_Wv': 8.0,
     'L1_attn_Wq': 4.105,
     'L1_ffn_fast_b': 8.0,
     'L1_ffn_w_fc': 8.0,
     'L1_ffn_w_proj': 8.0,
     'L1_ffn_u': 8.0,
     'L1_ffn_v': 8.0}
    for name, (base, spread) in spreads.items():
        noise = np.random.default_rng([zlib.crc32(name.encode()), seed]).standard_normal(out[name].shape)
        drawn = base * np.exp(spread * noise) if base else spread * noise
        out[name] = jnp.asarray(drawn.astype(out[name].dtype))
    for name, factor in factors.items():
        out[name] = (out[name] * factor).astype(out[name].dtype)
    return out
```

```python
from contextlib import ExitStack

import concourse.bass as bass
from concourse import mybir

F32 = mybir.dt.float32
BF16 = mybir.dt.bfloat16
ALU = mybir.AluOpType
ACT = mybir.ActivationFunctionType
AX = mybir.AxisListType

P = 128
EPS = 1e-5
Z_EPS = 1e-6
MIN_SCALE = 1e-5
RING = 3
PAIR_ROWS = 64
NEG_MAX_ROW = 48
STACK = [(0, 0), (0, 1), (0, 2), (1, 0), (1, 1), (2, 0)]
STACK_DMAS = 2 * 2 * len(STACK) + 2
AUG_DMAS = 4
SLOTS = 16
LEAD, TRAIL = 2, 2
MAX_TILES = [2, 2, 2, 2, 1, 1, 1, 1, 1, 1, 1, 1, 0, 0, 0, 0]
PT_RING = 8


class Seq:

    def __init__(self, const, turn=None):
        self.const, self.turn = const, turn
        self.ring = const % RING
        self.n = const if turn is None else turn * RING + const
        self.round = const // RING if turn is None else turn + const // RING

    def back(self, k):
        return Seq(self.const - k, self.turn)

    def follows(self, k):
        return self.turn is not None or self.const >= k

    def times(self, per, count=None):
        return self.n * per + (per if count is None else count)

    def landed(self, per):
        return (self.round + 1) * (16 * per)


def two_layer_kernel(nc, x, Wq, bq, Wk, bk, Wv, bv, Wp, bp, ffn_w, disha,
                     Wq1, bq1, Wk1, bk1, Wv1, bv1, Wc1, bc1, fast_b, w_fc, w_proj, u_fc, v_fc, gate, out):
    N, S, D = x.shape
    H, DK = 16, 8
    TT = S // P
    HID = w_fc.shape[0]
    HC = HID // P
    RK = fast_b.shape[0]
    RD = disha.shape[0]
    SCALE = 1.0 / DK ** 0.5
    PAIRS = H // 2
    assert D == P and TT == 2 and H * DK == D

    x_t = x.rearrange("n (t p) d -> n p t d", p=P)
    out_t = out.rearrange("n (t p) d -> n p t d", p=P)
    parts_dram = nc.dram_tensor("qk_parts", (RING, P, 3, 2, S), BF16, kind="Internal").ap()

    ctx = ExitStack()
    with ctx:
        def sb(name, shape, dt=F32):
            return ctx.enter_context(nc.sbuf_tensor(name, shape, dt))

        def psum(name):
            return ctx.enter_context(nc.psum_tensor(name, [P, 512], F32))

        def sem(name):
            return ctx.enter_context(nc.semaphore(name))

        ident = sb("ident", [P, P])
        ones_col = sb("ones_col", [P, 1])
        half_pow = sb("half_pow", [P, TT])
        head_mask = sb("head_mask", [P, H])
        block_mask = sb("block_mask", [P, P])
        zero_rows = sb("zero_rows", [2, PAIRS * S], BF16)
        raw = sb("raw", [P, 9, P])
        raw_fc = sb("raw_fc", [P, HC, P])
        raw_proj = sb("raw_proj", [P, HID])
        raw_u = sb("raw_u", [P, HC, P])
        raw_fb = sb("raw_fb", [P, P])
        raw_v = sb("raw_v", [RK, P])
        disha2 = sb("disha2", [P, P])
        wT = sb("wT", [P, 9, P])
        fcT = sb("fcT", [P, HID])
        projT = sb("projT", [P, HC, P])
        uT = sb("uT", [P, HID])
        fbT = sb("fbT", [P, P])
        fbv = sb("fbv", [RK, P])
        gate_col = sb("gate_col", [RK, 1])
        tern_pos = sb("tern_pos", [P, HID])
        tern_neg = sb("tern_neg", [P, HID])
        row_sum = sb("row_sum", [P, HC + 1])
        row_scale = sb("row_scale", [P, HC + 1])
        half_scale = sb("half_scale", [P, HC + 1])
        neg_half = sb("neg_half", [P, HC + 1])
        bias_col = sb("bias_col", [P, 3])
        bias_row = sb("bias_row", [P, 5, P])

        x_front = sb("x_front", [P, RING, TT, P])
        xn = {t: sb(f"xn_{t}", [P, TT, P]) for t in ("a0", "f0", "a1", "f1")}
        xnT = {t: sb(f"xnT_{t}", [P, S]) for t in ("a0", "f0", "a1", "f1")}
        stats = {t: sb(f"stats_{t}", [P, TT, 6]) for t in xn}
        mv = {t: sb(f"mv_{t}", [P, TT, 2]) for t in xn}
        var_eps = {t: sb(f"var_eps_{t}", [P, TT]) for t in xn}
        neg_mean = {t: sb(f"neg_mean_{t}", [P, TT]) for t in xn}
        rstd = {t: sb(f"rstd_{t}", [P, TT]) for t in xn}
        shift = {t: sb(f"shift_{t}", [P, TT]) for t in xn}
        qk = sb("qk", [P, 2, S])
        rest1 = sb("rest1", [P, 2, S])
        parts = sb("parts", [P, RING, 3, 2, S], BF16)
        q_stack = sb("q_stack", [P, RING, PAIRS, S], BF16)
        k_stack = sb("k_stack", [P, RING, H, S], BF16)
        v_hat = sb("v_hat", [P, RING, TT, H, 32])
        neg_max = sb("neg_max", [P, P])
        neg_max_parts = sb("neg_max_parts", [32, 2, P], BF16)
        probs = sb("probs", [P, PT_RING, TT, S])
        yT_raw = sb("yT_raw", [P, 2, S])
        inv_den = sb("inv_den", [P, TT * H])
        y0 = sb("y0", [P, TT * H, DK])
        x_mid = sb("x_mid", [P, RING, TT, P])
        x_bp = sb("x_bp", [P, TT, P])
        yT = sb("yT", [P, S])
        x1 = sb("x1", [P, TT, P])
        x2 = sb("x2", [P, TT, P])
        x2_bc = sb("x2_bc", [P, RING, TT, P])
        q1 = sb("q1", [P, S])
        q1_min = sb("q1_min", [P, S])
        q1_exp = sb("q1_exp", [P, S])
        q1_elu = sb("q1_elu", [P, S])
        k1 = sb("k1", [P, TT, P])
        k1_min = sb("k1_min", [P, TT, P])
        k1_exp = sb("k1_exp", [P, TT, P])
        k1_elu = sb("k1_elu", [P, TT, P])
        v1_ones = sb("v1_ones", [P, TT, P + 1])
        kv_blocks = sb("kv_blocks", [P, P + H])
        den1 = sb("den1", [P, TT, H])
        inv_den1 = sb("inv_den1", [P, TT, H])
        y1 = sb("y1", [P, TT, H, DK])
        y1T = sb("y1T", [P, RING, S])
        x3 = sb("x3", [P, TT, P])
        hid = sb("hid", [P, HC, S])
        hid2 = sb("hid2", [P, HC, S])
        x4 = sb("x4", [P, RING, TT, P])

        max_bank = [psum(f"max_bank{i}") for i in range(2)]
        score_bank = [psum(f"score_bank{i}") for i in range(2)]
        pv_bank = psum("pv_bank")
        front_bank = psum("front_bank")
        mid_bank = psum("mid_bank")
        last_bank = psum("last_bank")

        weights_in = sem("weights_in")
        pads_zero = sem("pads_zero")
        ident_made = sem("ident_made")
        consts_made = sem("consts_made")
        stacks_ready = sem("stacks_ready")
        prep_chain = sem("prep_chain")
        weight_turned = sem("weight_turned")
        weight_copied = sem("weight_copied")
        weights_ready = sem("weights_ready")
        x_in = [sem(f"x_in{r}") for r in range(RING)]
        x_mid_in = [sem(f"x_mid_in{r}") for r in range(RING)]
        parts_out = [sem(f"parts_out{r}") for r in range(RING)]
        stack_in = [sem(f"stack_in{r}") for r in range(RING)]
        aug_in = [sem(f"aug_in{r}") for r in range(RING)]
        out_done = [sem(f"out_done{r}") for r in range(RING)]
        ln_stats = {t: sem(f"ln_stats_{t}") for t in xn}
        ln_mv = {t: sem(f"ln_mv_{t}") for t in xn}
        ln_pre = {t: sem(f"ln_pre_{t}") for t in xn}
        ln_rstd = {t: sem(f"ln_rstd_{t}") for t in xn}
        ln_shift = {t: sem(f"ln_shift_{t}") for t in xn}
        ln_done = {t: sem(f"ln_done_{t}") for t in xn}
        xn_turned = {t: sem(f"xn_turned_{t}") for t in xn}
        xnT_done = {t: sem(f"xnT_done_{t}") for t in xn}
        qk_mm = sem("qk_mm")
        qk_done = sem("qk_done")
        v_mm = sem("v_mm")
        v_done = sem("v_done")
        split_done = sem("split_done")
        max_mm = sem("max_mm")
        max_done = sem("max_done")
        max_turned = sem("max_turned")
        max_parts = sem("max_parts")
        score_mm = sem("score_mm")
        exp_done = sem("exp_done")
        pv_mm = sem("pv_mm")
        yraw_done = sem("yraw_done")
        yraw_turned = sem("yraw_turned")
        den_done = sem("den_done")
        y0_done = sem("y0_done")
        y0_turned = sem("y0_turned")
        yT_done = sem("yT_done")
        xbp_done = sem("xbp_done")
        wp_mm = sem("wp_mm")
        x1_done = sem("x1_done")
        ffn_mm = sem("ffn_mm")
        x2_done = sem("x2_done")
        x2bc_done = sem("x2bc_done")
        kv1_mm = sem("kv1_mm")
        kv1_bias = sem("kv1_bias")
        q1_mm = sem("q1_mm")
        q1_bias = sem("q1_bias")
        q1_min_done = sem("q1_min_done")
        q1_exp_done = sem("q1_exp_done")
        q1_done = sem("q1_done")
        k1_min_done = sem("k1_min_done")
        k1_exp_done = sem("k1_exp_done")
        k1_done = sem("k1_done")
        state_mm = sem("state_mm")
        state_done = sem("state_done")
        y1_mm = sem("y1_mm")
        den1_done = sem("den1_done")
        y1_done = sem("y1_done")
        y1_turned = sem("y1_turned")
        y1T_done = sem("y1T_done")
        wc_mm = sem("wc_mm")
        x3_done = sem("x3_done")
        hid_mm = sem("hid_mm")
        hid_done = sem("hid_done")
        hid2_done = sem("hid2_done")
        proj_mm = sem("proj_mm")
        x4_done = sem("x4_done")
        dve_passed, pool_passed, sp_passed = sem("dve_passed"), sem("pool_passed"), sem("sp_passed")

        ternary_made, fbv_made, all_made = [0], [0], [0]

        block = ctx.enter_context(nc.Block())

        WQ, WK, WV, WP_, WF, WQ1, WK1, WV1, WC1 = range(9)
        square = [Wq, Wk, Wv, Wp, ffn_w, Wq1, Wk1, Wv1, Wc1]
        BV, BP, BK1, BV1, BC1 = range(5)
        WEIGHT_DMAS = 9 + 2 + 1 + 1 + 1 + 2 + 1 + 3 + 5

        def hold(eng, passed):
            eng.sem_inc(passed, 1)

        def run_steps(eng, step):
            def go(const, turn=None):
                def stage(off):
                    c = const + off
                    return Seq(c, turn) if turn is not None or 0 <= c < N else None
                step(stage(LEAD), stage(1), stage(0), stage(-1), stage(-TRAIL))
            loop_from = RING
            turns = (N - LEAD - loop_from) // RING
            for s in range(-LEAD, loop_from):
                go(s)
            with eng.Fori(0, turns) as turn:
                for k in range(RING):
                    go(loop_from + k, turn)
            for s in range(loop_from + turns * RING, N + TRAIL):
                go(s)

        @block.sync
        def _(sp):
            for i, w in enumerate(square):
                sp.dma_start(raw[:, i, :], w).then_inc(weights_in, 16)
            sp.dma_start(raw_fc[:, :, :], w_fc.rearrange("(c p) d -> p c d", p=P)).then_inc(weights_in, 16)
            sp.dma_start(raw_proj[:, :], w_proj).then_inc(weights_in, 16)
            sp.wait_ge(pads_zero, 2)
            sp.dma_start(raw_u[:, :, 0:RK], u_fc.rearrange("(c p) r -> p c r", p=P)).then_inc(weights_in, 16)
            sp.dma_start(raw_fb[0:RK, 0:RK], fast_b).then_inc(weights_in, 16)
            sp.dma_start(raw_v[:, :], v_fc).then_inc(weights_in, 16)
            for r in range(P // RD):
                sp.dma_start(disha2[r * RD:(r + 1) * RD, :], disha).then_inc(weights_in, 16)
            sp.dma_start(gate_col[:, :], gate.partition_broadcast(RK)).then_inc(weights_in, 16)
            for i, b in enumerate((bq, bk, bq1)):
                sp.dma_start(bias_col[:, i:i + 1], b.rearrange("(p a) -> p a", a=1)).then_inc(weights_in, 16)
            for i, b in enumerate((bv, bp, bk1, bv1, bc1)):
                sp.dma_start(bias_row[:, i, :], b.partition_broadcast(P)).then_inc(weights_in, 16)
            for n in range(LEAD):
                sp.dma_start(x_front[:, n, :, :], x_t[n]).then_inc(x_in[n], 16)
            sp.wait_ge(stacks_ready, 1)

            def step(front, maxima, heads, middle, last):
                if front:
                    if front.turn is not None or front.const + 1 < N:
                        nxt = front.back(-1)
                        if nxt.turn is not None or nxt.const >= LEAD:
                            if nxt.follows(RING):
                                sp.wait_ge(ln_done["a0"], nxt.back(RING).times(2))
                            if nxt.follows(RING):
                                sp.wait_ge(ln_stats["a0"], nxt.back(RING).times(2))
                            hold(sp, sp_passed)
                            sp.dma_start(x_front[:, nxt.ring, :, :], x_t[nxt.n]).then_inc(x_in[nxt.ring], 16)
                if heads:
                    if heads.follows(RING):
                        sp.wait_ge(xbp_done, heads.back(RING).times(1))
                    hold(sp, sp_passed)
                    sp.dma_start(x_mid[:, heads.ring, :, :], x_t[heads.n]).then_inc(x_mid_in[heads.ring], 16)
                if front:
                    f, r = front, front.ring
                    sp.wait_ge(split_done, f.times(4))
                    hold(sp, sp_passed)
                    if f.follows(RING):
                        sp.wait_ge(stack_in[f.ring], f.back(RING).landed(STACK_DMAS))
                    hold(sp, sp_passed)
                    sp.dma_start(parts_dram[r], parts[:, r]).then_inc(parts_out[r], 16)
                    sp.wait_ge(parts_out[f.ring], f.landed(1))
                    if f.follows(RING):
                        sp.wait_ge(score_mm, f.back(RING).times(H))
                    src = parts_dram[r].rearrange("(j h d) p a s -> h p a d j s", h=2, d=DK)
                    for half in range(2):
                        for i, (qp, kp) in enumerate(STACK):
                            a = half * PAIR_ROWS + i * DK
                            sp.dma_start(q_stack[a:a + DK, r, :, :], src[half, qp, 0]).then_inc(stack_in[r], 16)
                            sp.dma_start(k_stack[a:a + DK, r, half::2, :], src[half, kp, 1]).then_inc(stack_in[r], 16)
                        row = half * PAIR_ROWS + NEG_MAX_ROW
                        sp.dma_start(q_stack[row:row + 2, r, :, :], zero_rows[:, :].rearrange("p (j s) -> p j s", j=PAIRS)).then_inc(stack_in[r], 16)
                if last:
                    sp.wait_ge(x4_done, last.times(1))
                    hold(sp, sp_passed)
                    sp.dma_start(out_t[last.n], x4[:, last.ring, :, :]).then_inc(out_done[last.ring], 16)

            run_steps(sp, step)
            for n in range(N - RING, N):
                sp.wait_ge(out_done[Seq(n).ring], Seq(n).landed(1))

        @block.gpsimd
        def _(pool):
            pool.memset(ident[:, :], 0.0).then_inc(prep_chain, 1)
            pool.memset(block_mask[:, :], 1.0).then_inc(prep_chain, 1)
            pool.memset(head_mask[:, :], 1.0).then_inc(prep_chain, 1)
            pool.memset(raw_u[:, :, :], 0.0).then_inc(pads_zero, 1)
            pool.memset(raw_fb[:, :], 0.0).then_inc(pads_zero, 1)
            pool.wait_ge(prep_chain, 3)
            pool.affine_select(out=ident[:, :], in_=ident[:, :], compare_op=ALU.not_equal, fill=1.0, base=0,
                               pattern=[[-1, P]], channel_multiplier=1).then_inc(ident_made, 1)
            bm = block_mask[:, :].rearrange("p (h e) -> p h e", e=DK)
            pool.affine_select(out=bm, in_=bm, compare_op=ALU.is_ge, fill=0.0, base=0,
                               pattern=[[-DK, H], [0, DK]], channel_multiplier=1).then_inc(prep_chain, 1)
            pool.affine_select(out=head_mask[:, :], in_=head_mask[:, :], compare_op=ALU.is_ge, fill=0.0, base=0,
                               pattern=[[-DK, H]], channel_multiplier=1).then_inc(prep_chain, 1)
            pool.wait_ge(prep_chain, 5)
            pool.affine_select(out=bm, in_=bm, compare_op=ALU.is_ge, fill=0.0, base=DK - 1,
                               pattern=[[DK, H], [0, DK]], channel_multiplier=-1).then_inc(consts_made, 1)
            pool.affine_select(out=head_mask[:, :], in_=head_mask[:, :], compare_op=ALU.is_ge, fill=0.0, base=DK - 1,
                               pattern=[[DK, H]], channel_multiplier=-1).then_inc(consts_made, 1)
            pool.memset(half_pow[:, :], -0.5).then_inc(consts_made, 1)
            pool.wait_ge(consts_made, 3)

            def norm_scale(t, seq):
                pool.wait_ge(ln_mv[t], seq.times(2))
                if seq.follows(1):
                    pool.wait_ge(ln_done[t], seq.back(1).times(2))
                hold(pool, pool_passed)
                pool.tensor_scalar(var_eps[t][:, :], mv[t][:, :, 1], EPS, 1.0, ALU.add, ALU.mult).then_inc(ln_pre[t], 1)
                pool.tensor_scalar(neg_mean[t][:, :], mv[t][:, :, 0], -1.0, 1.0, ALU.mult, ALU.mult).then_inc(ln_pre[t], 1)
                pool.wait_ge(ln_pre[t], seq.times(2))
                pool.tensor_tensor(rstd[t][:, :], var_eps[t][:, :], half_pow[:, :], ALU.pow).then_inc(ln_rstd[t], 1)
                pool.wait_ge(ln_rstd[t], seq.times(1))
                pool.tensor_tensor(shift[t][:, :], neg_mean[t][:, :], rstd[t][:, :], ALU.mult).then_inc(ln_shift[t], 1)

            def step(front, maxima, heads, middle, last):
                for slot in range(SLOTS):
                    if front and slot == 0:
                        norm_scale("a0", front)
                    if middle and slot == 0:
                        m = middle
                        pool.wait_ge(x_mid_in[m.ring], m.landed(1))
                        if m.follows(1):
                            pool.wait_ge(x1_done, m.back(1).times(1))
                        pool.tensor_tensor(x_bp[:, 0, :], x_mid[:, m.ring, 0, :], bias_row[:, BP, :], ALU.add)
                        pool.tensor_tensor(x_bp[:, 1, :], x_mid[:, m.ring, 1, :], bias_row[:, BP, :], ALU.add).then_inc(xbp_done, 1)
                    if last and slot == 1:
                        norm_scale("f1", last)
                    if middle and slot == 2:
                        norm_scale("f0", middle)
                    if front and slot == 4:
                        f, r = front, front.ring
                        pool.wait_ge(qk_done, f.times(2))
                        if f.follows(RING):
                            pool.wait_ge(parts_out[f.ring], f.back(RING).landed(1))
                        hold(pool, pool_passed)
                        pool.tensor_scalar(parts[:, r, 0], qk[:, :, :], 1.0, 0.0, ALU.mult, ALU.add).then_inc(split_done, 1)
                        pool.wait_ge(split_done, f.times(4, 1))
                        pool.tensor_tensor(rest1[:, :, :], qk[:, :, :], parts[:, r, 0], ALU.subtract).then_inc(split_done, 1)
                        pool.wait_ge(split_done, f.times(4, 2))
                        hold(pool, pool_passed)
                        pool.tensor_scalar(parts[:, r, 1], rest1[:, :, :], 1.0, 0.0, ALU.mult, ALU.add).then_inc(split_done, 1)
                        pool.wait_ge(split_done, f.times(4, 3))
                        pool.tensor_tensor(parts[:, r, 2], rest1[:, :, :], parts[:, r, 1], ALU.subtract).then_inc(split_done, 1)
                    if last and slot in (5, 6):
                        l, c = last, slot - 5
                        pool.wait_ge(hid_done, l.times(2, c + 1))
                        if l.follows(1):
                            pool.wait_ge(proj_mm, l.back(1).times(1))
                        pool.tensor_tensor(hid2[:, 2 * c:2 * c + 2, :], hid[:, 2 * c:2 * c + 2, :], hid[:, 2 * c:2 * c + 2, :],
                                           ALU.mult).then_inc(hid2_done, 1)
                    if middle and slot == 6:
                        norm_scale("a1", middle)
                    if middle and slot == 7:
                        m = middle
                        pool.wait_ge(x2_done, m.times(1))
                        if m.follows(2):
                            pool.wait_ge(x3_done, m.back(2).times(1))
                        for t in range(TT):
                            ins = pool.tensor_tensor(x2_bc[:, m.ring, t, :], x2[:, t, :], bias_row[:, BC1, :], ALU.add)
                        ins.then_inc(x2bc_done, 1)

            run_steps(pool, step)

        @block.scalar
        def _(act):
            def normalise(t, seq, src):
                act.wait_ge(ln_shift[t], seq.times(1))
                if seq.follows(1):
                    act.wait_ge(xn_turned[t], seq.back(1).times(1))
                for i in range(TT):
                    nc.scalar.activation(xn[t][:, i, :], src[:, i, :], ACT.Identity, bias=shift[t][:, i:i + 1],
                                         scale=rstd[t][:, i:i + 1]).then_inc(ln_done[t], 1)

            def copy_turned(t, seq, bank, users):
                act.wait_ge(xn_turned[t], seq.times(1))
                for s in users:
                    if seq.follows(1):
                        act.wait_ge(s, seq.back(1).times(1))
                nc.scalar.activation(xnT[t][:, :], bank[:, 0:S], ACT.Copy).then_inc(xnT_done[t], 1)

            def step(front, maxima, heads, middle, last):
                for slot in range(SLOTS + 2):
                    if heads and slot < SLOTS:
                        n = heads.n * H + slot
                        act.wait_ge(score_mm, n + 1)
                        first = heads.turn is None and heads.const == 0 and slot < PT_RING
                        if not first:
                            act.wait_ge(pv_mm, heads.n * 4 + (slot - PT_RING) // 4 + 1)
                        nc.scalar.activation(probs[:, slot % PT_RING, :, :].rearrange("p t s -> p (t s)"),
                                             score_bank[slot % 2][:, :], ACT.Exp, scale=SCALE).then_inc(exp_done, 1)
                    if front and slot == 1:
                        act.wait_ge(x_in[front.ring], front.landed(1))
                        normalise("a0", front, x_front[:, front.ring])
                    if front and slot == 2:
                        copy_turned("a0", front, front_bank, (qk_mm, v_mm))
                    if front and slot == 3:
                        act.wait_ge(qk_mm, front.times(1))
                        if front.follows(1):
                            act.wait_ge(split_done, front.back(1).times(4))
                        for i in range(2):
                            nc.scalar.activation(qk[:, i, :], front_bank[:, i * S:(i + 1) * S], ACT.Identity,
                                                 bias=bias_col[:, i:i + 1]).then_inc(qk_done, 1)
                    if last and slot == 2:
                        normalise("f1", last, x3)
                    if last and slot == 3:
                        copy_turned("f1", last, last_bank, ())
                    if last and slot in (4, 5):
                        c = slot - 4
                        act.wait_ge(hid_mm, last.times(2, c + 1))
                        if last.follows(1):
                            act.wait_ge(hid2_done, last.back(1).times(2))
                        nc.scalar.activation(hid[:, 2 * c:2 * c + 2, :].rearrange("p c s -> p (c s)"), last_bank[:, :],
                                             ACT.Relu).then_inc(hid_done, 1)
                    if middle and slot == 0:
                        act.wait_ge(y0_turned, middle.times(1))
                        if middle.follows(1):
                            act.wait_ge(wp_mm, middle.back(1).times(1))
                        nc.scalar.activation(yT[:, :], mid_bank[:, 0:S], ACT.Copy).then_inc(yT_done, 1)
                    if middle and slot == 3:
                        normalise("f0", middle, x1)
                    if middle and slot == 4:
                        copy_turned("f0", middle, mid_bank, (ffn_mm,))
                    if middle and slot == 7:
                        normalise("a1", middle, x2)
                    if middle and slot == 8:
                        copy_turned("a1", middle, mid_bank, (kv1_mm, q1_mm))
                    if middle and slot == 10:
                        m = middle
                        act.wait_ge(k1_min_done, m.times(1))
                        if m.follows(1):
                            act.wait_ge(k1_done, m.back(1).times(1))
                        nc.scalar.activation(k1_exp[:, :, :], k1_min[:, :, :], ACT.Exp).then_inc(k1_exp_done, 1)
                        act.wait_ge(q1_mm, m.times(1))
                        if m.follows(1):
                            act.wait_ge(q1_done, m.back(1).times(1))
                        nc.scalar.activation(q1[:, :], mid_bank[:, 0:S], ACT.Identity, bias=bias_col[:, 2:3]).then_inc(q1_bias, 1)
                    if middle and slot == 11:
                        act.wait_ge(q1_min_done, middle.times(1))
                        nc.scalar.activation(q1_exp[:, :], q1_min[:, :], ACT.Exp).then_inc(q1_exp_done, 1)
                    if middle and slot == 15:
                        m = middle
                        act.wait_ge(y1_turned, m.times(1))
                        if m.follows(2):
                            act.wait_ge(wc_mm, m.back(2).times(1))
                        nc.scalar.activation(y1T[:, m.ring, :], mid_bank[:, 0:S], ACT.Copy).then_inc(y1T_done, 1)
                    if heads and slot == SLOTS + 1:
                        act.wait_ge(pv_mm, heads.times(4))
                        if heads.follows(1):
                            act.wait_ge(yraw_turned, heads.back(1).times(1))
                        nc.scalar.activation(yT_raw[:, :, :].rearrange("p b s -> p (b s)"), pv_bank[:, :], ACT.Copy).then_inc(yraw_done, 1)
                if maxima:
                    a, r = maxima, maxima.ring
                    act.wait_ge(max_parts, a.times(2))
                    for half in range(2):
                        for part in range(2):
                            row = half * PAIR_ROWS + NEG_MAX_ROW + part
                            act.dma_start(q_stack[row:row + 1, r, :, :].rearrange("p j (t s) -> p (j t) s", t=TT),
                                          neg_max_parts[16 * half:16 * half + 16, part, :]).then_inc(aug_in[r], 16)

            run_steps(act, step)

        @block.vector
        def _(dve):
            made = [0]

            def after(ins):
                ins.then_inc(weights_ready, 1)
                made[0] += 1
                dve.wait_ge(weights_ready, made[0])

            nc.vector.memset(k_stack[:, :, :, :], 0.0).then_inc(weights_ready, 1)
            nc.vector.memset(q_stack[:, :, :, :], 0.0).then_inc(weights_ready, 1)
            nc.vector.memset(v_hat[:, :, :, :, :], 0.0).then_inc(weights_ready, 1)
            nc.vector.memset(zero_rows[:, :], 0.0).then_inc(weights_ready, 1)
            nc.vector.memset(neg_max[:, :], 0.0).then_inc(weights_ready, 1)
            nc.vector.memset(v1_ones[:, :, :], 1.0).then_inc(weights_ready, 1)
            made[0] = 6
            dve.wait_ge(weights_ready, 6)
            for par in range(2):
                vh = v_hat[:, :, :, par::2, 16 * par + DK].rearrange("p r t h -> p (r t) h")
                after(nc.vector.memset(vh, 1.0))
            dve.wait_ge(ident_made, 1)
            dve.wait_ge(consts_made, 3)
            for half in range(2):
                c = half * PAIR_ROWS + NEG_MAX_ROW
                after(nc.vector.tensor_tensor(row_sum[:, half:half + 1], ident[:, c:c + 1], ident[:, c + 1:c + 2], ALU.add))
                dst = k_stack[:, :, half::2, :]
                for r in range(RING):
                    after(nc.vector.tensor_scalar(dst[:, r], dst[:, r], row_sum[:, half:half + 1], None, ALU.add))
            nc.vector.memset(ones_col[:, :], 1.0).then_inc(stacks_ready, 1)

            dve.wait_ge(weights_in, 16 * WEIGHT_DMAS)
            for c in range(HC + 1):
                src = raw_fc[:, c, :] if c < HC else raw_proj[:, :]
                after(nc.vector.tensor_reduce(row_sum[:, c:c + 1], src, AX.X, ALU.add, apply_absolute_value=True))
            after(nc.vector.tensor_scalar(row_scale[:, 0:HC], row_sum[:, 0:HC], 1.0 / D, MIN_SCALE, ALU.mult, ALU.max))
            after(nc.vector.tensor_scalar(row_scale[:, HC:HC + 1], row_sum[:, HC:HC + 1], 1.0 / HID, MIN_SCALE, ALU.mult, ALU.max))
            after(nc.vector.tensor_scalar(half_scale[:, :], row_scale[:, :], 0.5, None, ALU.mult))
            after(nc.vector.tensor_scalar(neg_half[:, :], row_scale[:, :], -0.5, None, ALU.mult))
            for c in range(HC + 1):
                src = raw_fc[:, c, :] if c < HC else raw_proj[:, :]
                w = src.shape[-1]
                after(nc.vector.tensor_scalar(tern_pos[:, 0:w], src, half_scale[:, c:c + 1], row_scale[:, c:c + 1], ALU.is_gt, ALU.mult))
                after(nc.vector.tensor_scalar(tern_neg[:, 0:w], src, neg_half[:, c:c + 1], row_scale[:, c:c + 1], ALU.is_lt, ALU.mult))
                after(nc.vector.tensor_tensor(src, tern_pos[:, 0:w], tern_neg[:, 0:w], ALU.subtract))
            ternary_made[0] = made[0]

            def turned(k):
                dve.wait_ge(weight_turned, k + 1)

            turned(0)
            nc.vector.tensor_copy(wT[:, 0:4, :], front_bank[:, :].rearrange("p (a b) -> p a b", a=4)).then_inc(weight_copied, 1)
            turned(1)
            nc.vector.tensor_copy(wT[:, 4:8, :], mid_bank[:, :].rearrange("p (a b) -> p a b", a=4)).then_inc(weight_copied, 1)
            turned(2)
            nc.vector.tensor_copy(wT[:, 8, :], last_bank[:, 0:P]).then_inc(weight_copied, 1)
            nc.vector.tensor_copy(fbT[:, :], last_bank[:, P:2 * P]).then_inc(weight_copied, 1)
            turned(3)
            nc.vector.tensor_copy(uT[:, :], pv_bank[:, :]).then_inc(weight_copied, 1)
            turned(4)
            nc.vector.tensor_copy(fcT[:, :], max_bank[0][:, :]).then_inc(weight_copied, 1)
            turned(5)
            nc.vector.tensor_copy(projT[:, :, :], max_bank[1][:, :].rearrange("p (a b) -> p a b", a=HC)).then_inc(weight_copied, 1)
            dve.wait_ge(weight_copied, 7)
            after(nc.vector.tensor_tensor(wT[:, WF, :], wT[:, WF, :], disha2[:, :], ALU.add))
            turned(6)
            after(nc.vector.tensor_scalar(fbv[:, :], score_bank[0][0:RK, 0:P], gate_col[:, 0:1], None, ALU.mult))
            fbv_made[0] = made[0]
            turned(7)
            after(nc.vector.tensor_tensor(fcT[:, :], score_bank[1][:, :], fcT[:, :], ALU.add))
            all_made[0] = made[0]

            def norm_stats(t, seq, src):
                if seq.follows(1):
                    dve.wait_ge(ln_mv[t], seq.back(1).times(2))
                for i in range(TT):
                    nc.vector.bn_stats(stats[t][:, i, :], src[:, i, :]).then_inc(ln_stats[t], 1)
                dve.wait_ge(ln_stats[t], seq.times(2))
                if seq.follows(1):
                    dve.wait_ge(ln_pre[t], seq.back(1).times(2))
                hold(dve, dve_passed)
                for i in range(TT):
                    nc.vector.bn_aggr(mv[t][:, i, :], stats[t][:, i, :]).then_inc(ln_mv[t], 1)

            def tile3(ap, b):
                return ap.rearrange("p (t d) -> p t d", t=b)

            def step(front, maxima, heads, middle, last):
                tile = 0
                if front:
                    dve.wait_ge(x_in[front.ring], front.landed(1))
                    norm_stats("a0", front, x_front[:, front.ring])
                for slot in range(SLOTS):
                    if maxima:
                        a = maxima
                        for _ in range(MAX_TILES[slot]):
                            t, j = tile // PAIRS, tile % PAIRS
                            dve.wait_ge(max_mm, a.n * 16 + tile + 1)
                            if tile == 0:
                                if a.follows(1):
                                    dve.wait_ge(max_turned, a.back(1).times(1))
                            dst = neg_max[:, 0:32].rearrange("p (h j t) -> p h j t", h=2, t=TT)[:, :, j, t]
                            nc.vector.tensor_reduce(dst, tile3(max_bank[tile % 2][:, :], 2), AX.X, ALU.max,
                                                    negate=True).then_inc(max_done, 1)
                            tile += 1
                        if slot == 12:
                            dve.wait_ge(max_turned, a.times(1))
                            if a.follows(1):
                                dve.wait_ge(aug_in[a.back(1).ring], a.back(1).landed(AUG_DMAS))
                            nc.vector.tensor_copy(neg_max_parts[:, 0, :], front_bank[0:32, 0:P]).then_inc(max_parts, 1)
                            dve.wait_ge(max_parts, a.times(2, 1))
                            nc.vector.tensor_tensor(neg_max_parts[:, 1, :], front_bank[0:32, 0:P], neg_max_parts[:, 0, :],
                                                    ALU.subtract).then_inc(max_parts, 1)
                    if last and slot == 0:
                        l = last
                        dve.wait_ge(wc_mm, l.times(1))
                        dve.wait_ge(x2bc_done, l.times(1))
                        if l.follows(1):
                            dve.wait_ge(x4_done, l.back(1).times(1))
                        if l.follows(1):
                            dve.wait_ge(ln_done["f1"], l.back(1).times(2))
                        nc.vector.tensor_tensor(x3[:, :, :], tile3(last_bank[:, 0:S], TT), x2_bc[:, l.ring], ALU.add).then_inc(x3_done, 1)
                        dve.wait_ge(x3_done, l.times(1))
                        norm_stats("f1", l, x3)
                    if last and slot == 9:
                        l = last
                        dve.wait_ge(proj_mm, l.times(1))
                        if l.follows(RING):
                            dve.wait_ge(out_done[l.ring], l.back(RING).landed(1))
                        nc.vector.tensor_tensor(x4[:, l.ring, :, :], tile3(last_bank[:, 0:S], TT), x3[:, :, :], ALU.add).then_inc(x4_done, 1)
                    if middle:
                        m = middle
                        if slot == 1:
                            dve.wait_ge(wp_mm, m.times(1))
                            dve.wait_ge(xbp_done, m.times(1))
                            if m.follows(1):
                                dve.wait_ge(x2_done, m.back(1).times(1))
                            if m.follows(1):
                                dve.wait_ge(ln_done["f0"], m.back(1).times(2))
                            nc.vector.tensor_tensor(x1[:, :, :], tile3(mid_bank[:, 0:S], TT), x_bp[:, :, :], ALU.add).then_inc(x1_done, 1)
                            dve.wait_ge(x1_done, m.times(1))
                            norm_stats("f0", m, x1)
                        if slot == 5:
                            dve.wait_ge(ffn_mm, m.times(1))
                            if m.follows(1):
                                dve.wait_ge(ln_done["a1"], m.back(1).times(2))
                            if m.follows(1):
                                dve.wait_ge(x2bc_done, m.back(1).times(1))
                            nc.vector.tensor_tensor(x2[:, :, :], tile3(mid_bank[:, 0:S], TT), x1[:, :, :], ALU.add).then_inc(x2_done, 1)
                            dve.wait_ge(x2_done, m.times(1))
                            norm_stats("a1", m, x2)
                        if slot == 9:
                            dve.wait_ge(kv1_mm, m.times(1))
                            if m.follows(1):
                                dve.wait_ge(k1_done, m.back(1).times(1))
                            if m.follows(1):
                                dve.wait_ge(state_mm, m.back(1).times(1))
                            kv = tile3(mid_bank[:, :], TT)
                            brow = bias_row[:, BK1:BV1 + 1, :]
                            nc.vector.tensor_tensor(k1[:, :, :], kv[:, :, 0:P], brow[:, 0:1, :].broadcast_to([P, TT, P]), ALU.add).then_inc(kv1_bias, 1)
                            nc.vector.tensor_tensor(v1_ones[:, :, 0:P], kv[:, :, P:2 * P], brow[:, 1:2, :].broadcast_to([P, TT, P]), ALU.add).then_inc(kv1_bias, 1)
                            dve.wait_ge(kv1_bias, m.times(2, 1))
                            if m.follows(1):
                                dve.wait_ge(k1_exp_done, m.back(1).times(1))
                            nc.vector.tensor_scalar(k1_min[:, :, :], k1[:, :, :], 0.0, None, ALU.min).then_inc(k1_min_done, 1)
                        if slot == 10:
                            dve.wait_ge(k1_exp_done, m.times(1))
                            if m.follows(1):
                                dve.wait_ge(state_mm, m.back(1).times(1))
                            nc.vector.scalar_tensor_tensor(k1_elu[:, :, :], k1[:, :, :], 0.0, k1_exp[:, :, :], ALU.max, ALU.add).then_inc(k1_done, 1)
                            dve.wait_ge(q1_bias, m.times(1))
                            if m.follows(1):
                                dve.wait_ge(q1_exp_done, m.back(1).times(1))
                            nc.vector.tensor_scalar(q1_min[:, :], q1[:, :], 0.0, None, ALU.min).then_inc(q1_min_done, 1)
                        if slot == 11:
                            dve.wait_ge(q1_exp_done, m.times(1))
                            if m.follows(1):
                                dve.wait_ge(y1_mm, m.back(1).times(1))
                            nc.vector.scalar_tensor_tensor(q1_elu[:, :], q1[:, :], 0.0, q1_exp[:, :], ALU.max, ALU.add).then_inc(q1_done, 1)
                        if slot == 12:
                            dve.wait_ge(state_mm, m.times(1))
                            if m.follows(1):
                                dve.wait_ge(y1_mm, m.back(1).times(1))
                            nc.vector.tensor_tensor(kv_blocks[:, 0:P], mid_bank[:, 0:P], block_mask[:, :], ALU.mult).then_inc(state_done, 1)
                            nc.vector.tensor_scalar(kv_blocks[:, P:P + H], head_mask[:, :], mid_bank[:, P:P + 1], None, ALU.mult).then_inc(state_done, 1)
                        if slot == 13:
                            dve.wait_ge(y1_mm, m.times(1))
                            if m.follows(1):
                                dve.wait_ge(y1_done, m.back(1).times(1))
                            y1p = tile3(mid_bank[:, 0:TT * (P + H)], TT)
                            nc.vector.tensor_scalar(den1[:, :, :], y1p[:, :, P:P + H], Z_EPS, None, ALU.add).then_inc(den1_done, 1)
                            dve.wait_ge(den1_done, m.times(2, 1))
                            nc.vector.reciprocal(inv_den1[:, :, :], den1[:, :, :]).then_inc(den1_done, 1)
                            dve.wait_ge(den1_done, m.times(2, 2))
                            if m.follows(1):
                                dve.wait_ge(y1_turned, m.back(1).times(1))
                            for t in range(TT):
                                ins = nc.vector.tensor_tensor(y1[:, t], y1p[:, t, 0:P].rearrange("p (h d) -> p h d", d=DK),
                                                              inv_den1[:, t, :].unsqueeze(2).broadcast_to([P, H, DK]), ALU.mult)
                            ins.then_inc(y1_done, 1)
                    if front and slot == 4:
                        f = front
                        dve.wait_ge(v_mm, f.times(1))
                        if f.follows(RING):
                            dve.wait_ge(pv_mm, f.back(RING).times(4))
                        for par in range(2):
                            dst = v_hat[:, f.ring, :, par::2, 16 * par:16 * par + DK]
                            src = front_bank[:, 0:S].rearrange("p (t h a d) -> p t h a d", t=TT, a=2, d=DK)[:, :, :, par, :]
                            b = bias_row[:, BV:BV + 1, :].rearrange("p o (h a d) -> p o h a d", a=2, d=DK)[:, :, :, par, :]
                            nc.vector.tensor_tensor(dst, src, b.broadcast_to([P, TT, PAIRS, DK]), ALU.add).then_inc(v_done, 1)
                if heads:
                    h = heads
                    dve.wait_ge(yraw_turned, h.times(1))
                    if h.follows(1):
                        dve.wait_ge(y0_turned, h.back(1).times(1))
                    heads_view = front_bank[:, :].rearrange("p (n c) -> p n c", c=16)
                    nc.vector.reciprocal(inv_den[:, :], heads_view[:, :, DK]).then_inc(den_done, 1)
                    dve.wait_ge(den_done, h.times(1))
                    nc.vector.tensor_tensor(y0[:, :, :], heads_view[:, :, 0:DK],
                                            inv_den[:, :].unsqueeze(2).broadcast_to([P, TT * H, DK]), ALU.mult).then_inc(y0_done, 1)

            run_steps(dve, step)

        @block.tensor
        def _(pe):
            pe.wait_ge(ident_made, 1)
            pe.wait_ge(weights_in, 16 * WEIGHT_DMAS)

            def turn_all(bank, srcs):
                for i, s in enumerate(srcs):
                    ins = nc.tensor.transpose(bank[:, i * P:(i + 1) * P], s, ident[:, :])
                ins.then_inc(weight_turned, 1)

            turn_all(front_bank, [raw[:, i, :] for i in range(4)])
            turn_all(mid_bank, [raw[:, i, :] for i in range(4, 8)])
            turn_all(last_bank, [raw[:, 8, :], raw_fb[:, :]])
            turn_all(pv_bank, [raw_u[:, c, :] for c in range(HC)])
            pe.wait_ge(weights_ready, ternary_made[0])
            turn_all(max_bank[0], [raw_fc[:, c, :] for c in range(HC)])
            turn_all(max_bank[1], [raw_proj[:, c * P:(c + 1) * P] for c in range(HC)])
            pe.wait_ge(weight_copied, 5)
            nc.tensor.matmul(score_bank[0][0:RK, 0:P], fbT[0:RK, 0:RK], raw_v[:, :], start=True, stop=True).then_inc(weight_turned, 1)
            pe.wait_ge(weights_ready, fbv_made[0])
            nc.tensor.matmul(score_bank[1][:, :], fbv[:, :], uT[0:RK, :], start=True, stop=True).then_inc(weight_turned, 1)
            pe.wait_ge(weights_ready, all_made[0])

            def turn_tokens(bank, src, signal):
                for t in range(TT):
                    ins = nc.tensor.transpose(bank[:, t * P:(t + 1) * P], src(t), ident[:, :])
                ins.then_inc(signal, 1)

            def by_token(bank, lhs, w, signal, width=P):
                for t in range(TT):
                    ins = nc.tensor.matmul(bank[:, t * width:(t + 1) * width], lhs[:, t * P:(t + 1) * P], w, start=True, stop=True)
                ins.then_inc(signal, 1)

            def pv(heads, g):
                v, b, a = heads.ring, g // 2, g % 2
                pe.wait_ge(exp_done, heads.n * H + 4 * g + 4)
                if g == 0:
                    if heads.follows(1):
                        pe.wait_ge(yraw_done, heads.back(1).times(1))
                for t in range(TT):
                    for j in range(4):
                        h = 8 * b + 2 * j + a
                        ins = nc.tensor.matmul(pv_bank[32 * j:32 * j + 32, b * S:(b + 1) * S], v_hat[:, v, t, h, :],
                                               probs[:, (4 * g + j) % PT_RING, t, :], start=(a == 0 and t == 0),
                                               stop=(a == 1 and t == TT - 1))
                ins.then_inc(pv_mm, 1)

            def step(front, maxima, heads, middle, last):
                tile = 0
                for slot in range(SLOTS):
                    if heads:
                        n, r = heads.n * H + slot, heads.ring
                        h = 8 * (slot // 8) + 2 * (slot % 4) + slot // 4 % 2
                        if slot == 0:
                            pe.wait_ge(aug_in[heads.ring], heads.landed(AUG_DMAS))
                        if not (heads.turn is None and heads.const == 0 and slot < 2):
                            pe.wait_ge(exp_done, n - 1)
                        for t in range(TT):
                            ins = nc.tensor.matmul(score_bank[slot % 2][:, t * S:(t + 1) * S], k_stack[:, r, h, t * P:(t + 1) * P],
                                                   q_stack[:, r, h // 2, :], start=True, stop=True)
                        ins.then_inc(score_mm, 1)
                    if maxima:
                        a, r = maxima, maxima.ring
                        if slot == 0:
                            pe.wait_ge(stack_in[a.ring], a.landed(STACK_DMAS))
                        for _ in range(MAX_TILES[slot]):
                            t, j = tile // PAIRS, tile % PAIRS
                            if not (a.turn is None and a.const == 0 and tile < 2):
                                pe.wait_ge(max_done, a.n * 16 + tile - 1)
                            nc.tensor.matmul(max_bank[tile % 2][:, :], q_stack[:, r, j, t * P:(t + 1) * P],
                                             k_stack[:, r, 2 * j:2 * j + 2, :].rearrange("p h s -> p (h s)"), start=True, stop=True).then_inc(max_mm, 1)
                            tile += 1
                        if slot == 12:
                            pe.wait_ge(max_done, a.times(16))
                            if front:
                                pe.wait_ge(v_done, front.times(2))
                            else:
                                if a.follows(2):
                                    pe.wait_ge(y0_done, a.back(2).times(1))
                            nc.tensor.transpose(front_bank[:, 0:P], neg_max[:, :], ident[:, :]).then_inc(max_turned, 1)
                    if heads and slot >= 5 and slot % 4 == 1:
                        pv(heads, slot // 4 - 1)
                    if last:
                        l = last
                        if slot == 0:
                            pe.wait_ge(y1T_done, l.times(1))
                            if l.follows(1):
                                pe.wait_ge(x4_done, l.back(1).times(1))
                            by_token(last_bank, y1T[:, l.ring, :], wT[:, WC1, :], wc_mm)
                        if slot == 3:
                            pe.wait_ge(ln_done["f1"], l.times(2))
                            pe.wait_ge(x3_done, l.times(1))
                            turn_tokens(last_bank, lambda t: xn["f1"][:, t, :], xn_turned["f1"])
                        if slot in (4, 5):
                            pe.wait_ge(xnT_done["f1"], l.times(1))
                            if slot == 5:
                                pe.wait_ge(hid_done, l.times(2, 1))
                            for i in range(2):
                                c = 2 * (slot - 4) + i
                                ins = nc.tensor.matmul(last_bank[:, i * S:(i + 1) * S], fcT[:, c * P:(c + 1) * P], xnT["f1"][:, :],
                                                       start=True, stop=True)
                            ins.then_inc(hid_mm, 1)
                        if slot == 9:
                            pe.wait_ge(hid2_done, l.times(2))
                            pe.wait_ge(hid_done, l.times(2))
                            for t in range(TT):
                                for c in range(HC):
                                    ins = nc.tensor.matmul(last_bank[:, t * P:(t + 1) * P], hid2[:, c, t * P:(t + 1) * P],
                                                           projT[:, c, :], start=(c == 0), stop=(c == HC - 1))
                            ins.then_inc(proj_mm, 1)
                    if middle:
                        m = middle
                        if slot == 0:
                            pe.wait_ge(y0_done, m.times(1))
                            if m.follows(1):
                                pe.wait_ge(y1T_done, m.back(1).times(1))
                            turn_tokens(mid_bank, lambda t: y0[:, t * H:(t + 1) * H, :].rearrange("p h d -> p (h d)"), y0_turned)
                        if slot == 1:
                            pe.wait_ge(yT_done, m.times(1))
                            by_token(mid_bank, yT, wT[:, WP_, :], wp_mm)
                        if slot == 4:
                            pe.wait_ge(ln_done["f0"], m.times(2))
                            turn_tokens(mid_bank, lambda t: xn["f0"][:, t, :], xn_turned["f0"])
                        if slot == 5:
                            pe.wait_ge(xnT_done["f0"], m.times(1))
                            by_token(mid_bank, xnT["f0"], wT[:, WF, :], ffn_mm)
                        if slot == 8:
                            pe.wait_ge(ln_done["a1"], m.times(2))
                            turn_tokens(mid_bank, lambda t: xn["a1"][:, t, :], xn_turned["a1"])
                        if slot == 9:
                            pe.wait_ge(xnT_done["a1"], m.times(1))
                            by_token(mid_bank, xnT["a1"], wT[:, WK1:WV1 + 1, :].rearrange("p a b -> p (a b)"), kv1_mm, 2 * P)
                        if slot == 10:
                            pe.wait_ge(kv1_bias, m.times(2))
                            nc.tensor.matmul(mid_bank[:, 0:S], wT[:, WQ1, :], xnT["a1"][:, :], start=True, stop=True).then_inc(q1_mm, 1)
                        if slot == 12:
                            pe.wait_ge(k1_done, m.times(1))
                            pe.wait_ge(q1_bias, m.times(1))
                            for t in range(TT):
                                ins = nc.tensor.matmul(mid_bank[:, 0:P + 1], k1_elu[:, t, :], v1_ones[:, t, :], start=(t == 0), stop=(t == TT - 1))
                            ins.then_inc(state_mm, 1)
                        if slot == 13:
                            pe.wait_ge(state_done, m.times(2))
                            pe.wait_ge(q1_done, m.times(1))
                            by_token(mid_bank, q1_elu, kv_blocks[:, :], y1_mm, P + H)
                        if slot == 15:
                            pe.wait_ge(y1_done, m.times(1))
                            turn_tokens(mid_bank, lambda t: y1[:, t].rearrange("p h d -> p (h d)"), y1_turned)
                    if front:
                        f = front
                        if slot == 2:
                            pe.wait_ge(ln_done["a0"], f.times(2))
                            if f.follows(3):
                                pe.wait_ge(y0_done, f.back(3).times(1))
                            turn_tokens(front_bank, lambda t: xn["a0"][:, t, :], xn_turned["a0"])
                        if slot == 3:
                            pe.wait_ge(xnT_done["a0"], f.times(1))
                            for i, w in enumerate((WQ, WK)):
                                ins = nc.tensor.matmul(front_bank[:, i * S:(i + 1) * S], wT[:, w, :], xnT["a0"][:, :], start=True, stop=True)
                            ins.then_inc(qk_mm, 1)
                        if slot == 4:
                            pe.wait_ge(qk_done, f.times(2))
                            by_token(front_bank, xnT["a0"], wT[:, WV, :], v_mm)
                if heads:
                    pv(heads, 3)
                    pe.wait_ge(yraw_done, heads.times(1))
                    if maxima:
                        pe.wait_ge(max_parts, maxima.times(2))
                    for t in range(TT):
                        for b in range(2):
                            ins = nc.tensor.transpose(front_bank[:, (2 * t + b) * P:(2 * t + b + 1) * P],
                                                      yT_raw[:, b, t * P:(t + 1) * P], ident[:, :])
                    ins.then_inc(yraw_turned, 1)

            run_steps(pe, step)


_INS = ['L0_attn_x', 'L0_attn_Wq', 'L0_attn_bq', 'L0_attn_Wk', 'L0_attn_bk', 'L0_attn_Wv', 'L0_attn_bv',
        'L0_attn_Wp', 'L0_attn_bp', 'L0_ffn_weight', 'L0_ffn_disha', 'L1_attn_Wq', 'L1_attn_bq', 'L1_attn_Wk',
        'L1_attn_bk', 'L1_attn_Wv', 'L1_attn_bv', 'L1_attn_Wc', 'L1_attn_bc', 'L1_ffn_fast_b', 'L1_ffn_w_fc',
        'L1_ffn_w_proj', 'L1_ffn_u', 'L1_ffn_v', 'L1_ffn_gate']


def kernel(**inputs):
    import numpy as _np
    import concourse.bacc as _bacc
    from concourse import mybir as _mybir
    from concourse.bass_utils import run_bass_kernel_spmd as _run

    nc = _bacc.Bacc("TRN2", target_bir_lowering=False, num_devices=1)
    arrays, args = {}, []
    for name in _INS:
        a = _np.ascontiguousarray(inputs[name])
        if a.ndim == 0:
            a = a.reshape(1)
        arrays[f"in_{name}_dram"] = a
        args.append(nc.dram_tensor(f"in_{name}_dram", a.shape, _mybir.dt.from_np(a.dtype), kind="ExternalInput").ap())
    shape = arrays["in_L0_attn_x_dram"].shape
    args.append(nc.dram_tensor("out_0_dram", shape, _mybir.dt.float32, kind="ExternalOutput").ap())
    two_layer_kernel(nc, *args)
    r = _run(nc, [arrays], core_ids=[0])
    return r.results[0]["out_0_dram"]
```

```python
from contextlib import ExitStack

import concourse.bass as bass
from concourse import mybir

F32 = mybir.dt.float32
BF16 = mybir.dt.bfloat16
ALU = mybir.AluOpType
ACT = mybir.ActivationFunctionType
AX = mybir.AxisListType

P = 128
EPS = 1e-5
Z_EPS = 1e-6
MIN_SCALE = 1e-5
RING = 3
PAIR_ROWS = 64
NEG_MAX_ROW = 48
RUNS = [(3, 0, 0), (2, 0, 1), (1, 0, 2)]
PARTS_DMAS = 3 * 2
STACK_DMAS = 2 * 2 * len(RUNS) + 2
AUG_DMAS = 4
SLOTS = 16
TAIL = SLOTS
LEAD, TRAIL = 3, 2
MAX_TILES = [0, 0, 2, 1, 2, 1, 2, 1, 2, 1, 1, 1, 1, 1, 0, 0]
PT_RING = 8


class Seq:

    def __init__(self, const, turn=None):
        self.const, self.turn = const, turn
        self.ring = const % RING
        self.n = const if turn is None else turn * RING + const
        self.round = const // RING if turn is None else turn + const // RING

    def back(self, k):
        return Seq(self.const - k, self.turn)

    def follows(self, k):
        return self.turn is not None or self.const >= k

    def times(self, per, count=None):
        return self.n * per + (per if count is None else count)

    def landed(self, per):
        return (self.round + 1) * (16 * per)


def two_layer_kernel(nc, x, Wq, bq, Wk, bk, Wv, bv, Wp, bp, ffn_w, disha,
                     Wq1, bq1, Wk1, bk1, Wv1, bv1, Wc1, bc1, fast_b, w_fc, w_proj, u_fc, v_fc, gate, out):
    N, S, D = x.shape
    H, DK = 16, 8
    TT = S // P
    HID = w_fc.shape[0]
    HC = HID // P
    RK = fast_b.shape[0]
    RD = disha.shape[0]
    SCALE = 1.0 / DK ** 0.5
    PAIRS = H // 2
    assert D == P and TT == 2 and H * DK == D

    x_t = x.rearrange("n (t p) d -> n p t d", p=P)
    out_t = out.rearrange("n (t p) d -> n p t d", p=P)
    parts_dram = nc.dram_tensor("qk_parts", (RING, PAIRS, 2, 2, 3, DK, S), BF16, kind="Internal").ap()

    ctx = ExitStack()
    with ctx:
        def sb(name, shape, dt=F32):
            return ctx.enter_context(nc.sbuf_tensor(name, shape, dt))

        def psum(name):
            return ctx.enter_context(nc.psum_tensor(name, [P, 512], F32))

        def sem(name):
            return ctx.enter_context(nc.semaphore(name))

        ident = sb("ident", [P, P])
        ones_col = sb("ones_col", [P, 1])
        half_pow = sb("half_pow", [P, TT])
        head_mask = sb("head_mask", [P, H])
        block_mask = sb("block_mask", [P, P])
        zero_rows = sb("zero_rows", [2, PAIRS * S], BF16)
        one_rows = sb("one_rows", [2, RING * PAIRS * S], BF16)
        raw = sb("raw", [P, 9, P])
        raw_fc = sb("raw_fc", [P, HC, P])
        raw_proj = sb("raw_proj", [P, HID])
        raw_u = sb("raw_u", [P, HC, P])
        raw_fb = sb("raw_fb", [P, P])
        raw_v = sb("raw_v", [RK, P])
        disha2 = sb("disha2", [P, P])
        wT = sb("wT", [P, 9, P])
        fcT = sb("fcT", [P, HID])
        projT = sb("projT", [P, HC, P])
        uT = sb("uT", [P, HID])
        fbT = sb("fbT", [P, P])
        fbv = sb("fbv", [RK, P])
        gate_col = sb("gate_col", [RK, 1])
        tern_pos = sb("tern_pos", [P, HID])
        tern_neg = sb("tern_neg", [P, HID])
        row_sum = sb("row_sum", [P, HC + 1])
        row_scale = sb("row_scale", [P, HC + 1])
        half_scale = sb("half_scale", [P, HC + 1])
        neg_half = sb("neg_half", [P, HC + 1])
        bias_col = sb("bias_col", [P, 3])
        bias_row = sb("bias_row", [P, 5, P])

        x_front = sb("x_front", [P, RING, TT, P])
        xn = {t: sb(f"xn_{t}", [P, TT, P]) for t in ("a0", "f0", "a1", "f1")}
        xnT = {t: sb(f"xnT_{t}", [P, S]) for t in ("a0", "f0", "a1", "f1")}
        stats = {t: sb(f"stats_{t}", [P, TT, 6]) for t in xn}
        mv = {t: sb(f"mv_{t}", [P, TT, 2]) for t in xn}
        var_eps = {t: sb(f"var_eps_{t}", [P, TT]) for t in xn}
        neg_mean = {t: sb(f"neg_mean_{t}", [P, TT]) for t in xn}
        rstd = {t: sb(f"rstd_{t}", [P, TT]) for t in xn}
        shift = {t: sb(f"shift_{t}", [P, TT]) for t in xn}
        qk = sb("qk", [P, 2, S])
        rest = [sb(f"rest{i}", [P, 2, S]) for i in range(2)]
        parts = sb("parts", [P, RING, 3, 2, S], BF16)
        q_stack = sb("q_stack", [P, RING, PAIRS, S], BF16)
        k_stack = sb("k_stack", [P, RING, H, S], BF16)
        v_hat = sb("v_hat", [P, RING, TT, H, 32])
        neg_max = sb("neg_max", [P, P])
        neg_max_parts = sb("neg_max_parts", [32, 2, P], BF16)
        probs = sb("probs", [P, PT_RING, TT, S])
        yT_raw = sb("yT_raw", [P, 2, S])
        inv_den = sb("inv_den", [P, TT * H])
        y0 = sb("y0", [P, TT * H, DK])
        x_mid = sb("x_mid", [P, RING, TT, P])
        x_bp = sb("x_bp", [P, TT, P])
        yT = sb("yT", [P, S])
        x1 = sb("x1", [P, TT, P])
        x2 = sb("x2", [P, TT, P])
        x2_bc = sb("x2_bc", [P, TT, P])
        q1 = sb("q1", [P, S])
        q1_min = sb("q1_min", [P, S])
        q1_exp = sb("q1_exp", [P, S])
        q1_elu = sb("q1_elu", [P, S])
        k1 = sb("k1", [P, TT, P])
        k1_min = sb("k1_min", [P, TT, P])
        k1_exp = sb("k1_exp", [P, TT, P])
        k1_elu = sb("k1_elu", [P, TT, P])
        v1_ones = sb("v1_ones", [P, TT, P + 1])
        kv_blocks = sb("kv_blocks", [P, P + H])
        den1 = sb("den1", [P, TT, H])
        inv_den1 = sb("inv_den1", [P, TT, H])
        y1 = sb("y1", [P, TT, H, DK])
        y1T = sb("y1T", [P, S])
        x3 = sb("x3", [P, TT, P])
        hid = sb("hid", [P, HC, S])
        hid2 = sb("hid2", [P, HC, S])
        x4 = sb("x4", [P, RING, TT, P])

        max_bank = [psum(f"max_bank{i}") for i in range(2)]
        score_bank = [psum(f"score_bank{i}") for i in range(2)]
        pv_bank = psum("pv_bank")
        front_bank = psum("front_bank")
        mid_bank = psum("mid_bank")
        last_bank = psum("last_bank")

        first_in = sem("first_in")
        weights_in = sem("weights_in")
        ones_in = sem("ones_in")
        small_made = sem("small_made")
        pads_zero = sem("pads_zero")
        ident_made = sem("ident_made")
        consts_made = sem("consts_made")
        stacks_ready = sem("stacks_ready")
        prep_chain = sem("prep_chain")
        weight_turned = sem("weight_turned")
        weight_copied = sem("weight_copied")
        weights_ready = sem("weights_ready")
        x_in = [sem(f"x_in{r}") for r in range(RING)]
        x_mid_in = [sem(f"x_mid_in{r}") for r in range(RING)]
        parts_out = [sem(f"parts_out{r}") for r in range(RING)]
        stack_in = [sem(f"stack_in{r}") for r in range(RING)]
        aug_in = [sem(f"aug_in{r}") for r in range(RING)]
        out_done = [sem(f"out_done{r}") for r in range(RING)]
        ln_stats = {t: sem(f"ln_stats_{t}") for t in xn}
        ln_mv = {t: sem(f"ln_mv_{t}") for t in xn}
        ln_pre = {t: sem(f"ln_pre_{t}") for t in xn}
        ln_rstd = {t: sem(f"ln_rstd_{t}") for t in xn}
        ln_shift = {t: sem(f"ln_shift_{t}") for t in xn}
        ln_done = {t: sem(f"ln_done_{t}") for t in xn}
        xn_turned = {t: sem(f"xn_turned_{t}") for t in xn}
        xnT_done = {t: sem(f"xnT_done_{t}") for t in xn}
        qk_mm = sem("qk_mm")
        qk_done = sem("qk_done")
        v_mm = sem("v_mm")
        v_done = sem("v_done")
        split_done = sem("split_done")
        max_mm = sem("max_mm")
        max_done = sem("max_done")
        max_turned = sem("max_turned")
        max_parts = sem("max_parts")
        score_mm = sem("score_mm")
        exp_done = sem("exp_done")
        pv_mm = sem("pv_mm")
        yraw_done = sem("yraw_done")
        yraw_turned = sem("yraw_turned")
        den_done = sem("den_done")
        y0_done = sem("y0_done")
        y0_turned = sem("y0_turned")
        yT_done = sem("yT_done")
        xbp_done = sem("xbp_done")
        wp_mm = sem("wp_mm")
        x1_done = sem("x1_done")
        ffn_mm = sem("ffn_mm")
        x2_done = sem("x2_done")
        x2bc_done = sem("x2bc_done")
        kv1_mm = sem("kv1_mm")
        kv1_bias = sem("kv1_bias")
        q1_mm = sem("q1_mm")
        q1_bias = sem("q1_bias")
        q1_min_done = sem("q1_min_done")
        q1_exp_done = sem("q1_exp_done")
        q1_done = sem("q1_done")
        k1_min_done = sem("k1_min_done")
        k1_exp_done = sem("k1_exp_done")
        k1_done = sem("k1_done")
        state_mm = sem("state_mm")
        state_done = sem("state_done")
        y1_mm = sem("y1_mm")
        den1_done = sem("den1_done")
        y1_done = sem("y1_done")
        y1_turned = sem("y1_turned")
        y1T_done = sem("y1T_done")
        wc_mm = sem("wc_mm")
        x3_done = sem("x3_done")
        hid_mm = sem("hid_mm")
        hid_done = sem("hid_done")
        hid2_done = sem("hid2_done")
        proj_mm = sem("proj_mm")
        x4_done = sem("x4_done")
        dve_passed, pool_passed, sp_passed = sem("dve_passed"), sem("pool_passed"), sem("sp_passed")

        ternary_made, fbv_made, all_made = [0], [0], [0]

        block = ctx.enter_context(nc.Block())

        WQ, WK, WV, WP_, WF, WQ1, WK1, WV1, WC1 = range(9)
        square = [Wq, Wk, Wv, Wp, ffn_w, Wq1, Wk1, Wv1, Wc1]
        BV, BP, BK1, BV1, BC1 = range(5)
        FIRST_DMAS = 3 + 2 + 1
        WEIGHT_DMAS = 6 + 2 + 1 + 1 + 1 + 2 + 1 + 1 + 4

        def hold(eng, passed):
            eng.sem_inc(passed, 1)

        def run_steps(eng, step, before={}):
            def go(const, turn=None):
                def stage(off):
                    c = const + off
                    return Seq(c, turn) if turn is not None or 0 <= c < N else None
                step(stage(LEAD), stage(2), stage(1), stage(0), stage(-1), stage(-TRAIL))
            loop_from = RING
            turns = (N - LEAD - loop_from) // RING
            for s in range(-LEAD, loop_from):
                if s in before:
                    before[s]()
                go(s)
            with eng.Fori(0, turns) as turn:
                for k in range(RING):
                    go(loop_from + k, turn)
            for s in range(loop_from + turns * RING, N + TRAIL):
                go(s)

        @block.sync
        def _(sp):
            sp.dma_start(x_front[:, 0, :, :], x_t[0]).then_inc(x_in[0], 16)
            for i in (WQ, WK, WV):
                sp.dma_start(raw[:, i, :], square[i]).then_inc(first_in, 16)
            for i, b in enumerate((bq, bk)):
                sp.dma_start(bias_col[:, i:i + 1], b.rearrange("(p a) -> p a", a=1)).then_inc(first_in, 16)
            sp.dma_start(bias_row[:, BV, :], bv.partition_broadcast(P)).then_inc(first_in, 16)
            for i in range(WP_, WC1 + 1):
                sp.dma_start(raw[:, i, :], square[i]).then_inc(weights_in, 16)
            sp.dma_start(raw_fc[:, :, :], w_fc.rearrange("(c p) d -> p c d", p=P)).then_inc(weights_in, 16)
            sp.dma_start(raw_proj[:, :], w_proj).then_inc(weights_in, 16)
            sp.wait_ge(pads_zero, 2)
            sp.dma_start(raw_u[:, :, 0:RK], u_fc.rearrange("(c p) r -> p c r", p=P)).then_inc(weights_in, 16)
            sp.dma_start(raw_fb[0:RK, 0:RK], fast_b).then_inc(weights_in, 16)
            sp.dma_start(raw_v[:, :], v_fc).then_inc(weights_in, 16)
            for i in range(P // RD):
                sp.dma_start(disha2[i * RD:(i + 1) * RD, :], disha).then_inc(weights_in, 16)
            sp.dma_start(gate_col[:, :], gate.partition_broadcast(RK)).then_inc(weights_in, 16)
            sp.dma_start(bias_col[:, 2:3], bq1.rearrange("(p a) -> p a", a=1)).then_inc(weights_in, 16)
            for i, b in ((BP, bp), (BK1, bk1), (BV1, bv1), (BC1, bc1)):
                sp.dma_start(bias_row[:, i, :], b.partition_broadcast(P)).then_inc(weights_in, 16)

            def rows_of_ones():
                sp.wait_ge(stacks_ready, 4)
                for half in range(2):
                    row = half * PAIR_ROWS + NEG_MAX_ROW
                    sp.dma_start(k_stack[row:row + 2, :, half::2, :].rearrange("p r j s -> p (r j) s"),
                                 one_rows[:, :].rearrange("p (n s) -> p n s", s=S)).then_inc(ones_in, 16)

            def step(ahead, front, maxima, heads, middle, last):
                if ahead and (ahead.turn is not None or ahead.const + 1 < N):
                    nxt = ahead.back(-1)
                    if nxt.follows(RING):
                        sp.wait_ge(ln_done["a0"], nxt.back(RING).times(2))
                        sp.wait_ge(ln_stats["a0"], nxt.back(RING).times(2))
                        hold(sp, sp_passed)
                    sp.dma_start(x_front[:, nxt.ring, :, :], x_t[nxt.n]).then_inc(x_in[nxt.ring], 16)
                if heads:
                    if heads.follows(RING):
                        sp.wait_ge(xbp_done, heads.back(RING).times(1))
                        hold(sp, sp_passed)
                    sp.dma_start(x_mid[:, heads.ring, :, :], x_t[heads.n]).then_inc(x_mid_in[heads.ring], 16)
                if front:
                    f, r = front, front.ring
                    if f.follows(RING):
                        sp.wait_ge(stack_in[r], f.back(RING).landed(STACK_DMAS))
                        hold(sp, sp_passed)
                    for part in range(3):
                        sp.wait_ge(split_done, f.times(5, (1, 3, 5)[part]))
                        hold(sp, sp_passed)
                        for a in range(2):
                            place = part if a == 0 else 2 - part
                            sp.dma_start(parts_dram[r, :, :, a, place].rearrange("j h d s -> (j h) d s"),
                                         parts[:, r, part, a, :]).then_inc(parts_out[r], 16)
                    sp.wait_ge(parts_out[r], f.landed(PARTS_DMAS))
                    if f.follows(RING):
                        sp.wait_ge(score_mm, f.back(RING).times(H))
                    for half in range(2):
                        row = half * PAIR_ROWS
                        for run, q_place, k_place in RUNS:
                            end = row + run * DK
                            sp.dma_start(q_stack[row:end, r, :, :],
                                         parts_dram[r, :, half, 0, q_place:q_place + run].rearrange("j n d s -> (n d) j s")).then_inc(stack_in[r], 16)
                            sp.dma_start(k_stack[row:end, r, half::2, :],
                                         parts_dram[r, :, half, 1, k_place:k_place + run].rearrange("j n d s -> (n d) j s")).then_inc(stack_in[r], 16)
                            row = end
                        sp.dma_start(q_stack[row:row + 2, r, :, :],
                                     zero_rows[:, :].rearrange("p (j s) -> p j s", j=PAIRS)).then_inc(stack_in[r], 16)
                if last:
                    sp.wait_ge(x4_done, last.times(1))
                    hold(sp, sp_passed)
                    sp.dma_start(out_t[last.n], x4[:, last.ring, :, :]).then_inc(out_done[last.ring], 16)

            run_steps(sp, step, {-2: rows_of_ones})
            for n in range(N - RING, N):
                sp.wait_ge(out_done[Seq(n).ring], Seq(n).landed(1))

        @block.gpsimd
        def _(pool):
            pool.memset(ident[:, :], 0.0).then_inc(prep_chain, 1)
            pool.memset(half_pow[:, :], -0.5).then_inc(prep_chain, 1)
            pool.wait_ge(prep_chain, 2)
            pool.affine_select(out=ident[:, :], in_=ident[:, :], compare_op=ALU.not_equal, fill=1.0, base=0,
                               pattern=[[-1, P]], channel_multiplier=1).then_inc(ident_made, 1)
            pool.memset(raw_u[:, :, :], 0.0).then_inc(pads_zero, 1)
            pool.memset(raw_fb[:, :], 0.0).then_inc(pads_zero, 1)

            def masks():
                pool.memset(block_mask[:, :], 1.0).then_inc(prep_chain, 1)
                pool.memset(head_mask[:, :], 1.0).then_inc(prep_chain, 1)
                pool.wait_ge(prep_chain, 4)
                bm = block_mask[:, :].rearrange("p (h e) -> p h e", e=DK)
                pool.affine_select(out=bm, in_=bm, compare_op=ALU.is_ge, fill=0.0, base=0,
                                   pattern=[[-DK, H], [0, DK]], channel_multiplier=1).then_inc(prep_chain, 1)
                pool.affine_select(out=head_mask[:, :], in_=head_mask[:, :], compare_op=ALU.is_ge, fill=0.0, base=0,
                                   pattern=[[-DK, H]], channel_multiplier=1).then_inc(prep_chain, 1)
                pool.wait_ge(prep_chain, 6)
                pool.affine_select(out=bm, in_=bm, compare_op=ALU.is_ge, fill=0.0, base=DK - 1,
                                   pattern=[[DK, H], [0, DK]], channel_multiplier=-1).then_inc(consts_made, 1)
                pool.affine_select(out=head_mask[:, :], in_=head_mask[:, :], compare_op=ALU.is_ge, fill=0.0, base=DK - 1,
                                   pattern=[[DK, H]], channel_multiplier=-1).then_inc(consts_made, 1)
                pool.wait_ge(weights_in, 16 * WEIGHT_DMAS)

            def norm_scale(t, seq):
                pool.wait_ge(ln_mv[t], seq.times(2))
                if seq.follows(1):
                    pool.wait_ge(ln_done[t], seq.back(1).times(2))
                hold(pool, pool_passed)
                pool.tensor_scalar(var_eps[t][:, :], mv[t][:, :, 1], EPS, 1.0, ALU.add, ALU.mult).then_inc(ln_pre[t], 1)
                pool.tensor_scalar(neg_mean[t][:, :], mv[t][:, :, 0], -1.0, 1.0, ALU.mult, ALU.mult).then_inc(ln_pre[t], 1)
                pool.wait_ge(ln_pre[t], seq.times(2))
                pool.tensor_tensor(rstd[t][:, :], var_eps[t][:, :], half_pow[:, :], ALU.pow).then_inc(ln_rstd[t], 1)
                pool.wait_ge(ln_rstd[t], seq.times(1))
                pool.tensor_tensor(shift[t][:, :], neg_mean[t][:, :], rstd[t][:, :], ALU.mult).then_inc(ln_shift[t], 1)

            def split(f, i):
                r = f.ring
                left = qk if i == 0 else rest[i - 1]
                if i == 0:
                    pool.wait_ge(qk_done, f.times(2))
                    if f.follows(RING):
                        pool.wait_ge(parts_out[r], f.back(RING).landed(PARTS_DMAS))
                else:
                    pool.wait_ge(split_done, f.times(5, 2 * i))
                hold(pool, pool_passed)
                pool.tensor_scalar(parts[:, r, i], left[:, :, :], 1.0, 0.0, ALU.mult, ALU.add).then_inc(split_done, 1)
                if i < 2:
                    pool.wait_ge(split_done, f.times(5, 2 * i + 1))
                    pool.tensor_tensor(rest[i][:, :, :], left[:, :, :], parts[:, r, i], ALU.subtract).then_inc(split_done, 1)

            def step(ahead, front, maxima, heads, middle, last):
                for slot in range(SLOTS + 1):
                    if middle and slot == 0:
                        m = middle
                        pool.wait_ge(x_mid_in[m.ring], m.landed(1))
                        if m.follows(1):
                            pool.wait_ge(x1_done, m.back(1).times(1))
                        pool.tensor_tensor(x_bp[:, 0, :], x_mid[:, m.ring, 0, :], bias_row[:, BP, :], ALU.add)
                        pool.tensor_tensor(x_bp[:, 1, :], x_mid[:, m.ring, 1, :], bias_row[:, BP, :], ALU.add).then_inc(xbp_done, 1)
                    if front and slot == 1:
                        split(front, 0)
                    if middle and slot == 2:
                        norm_scale("f0", middle)
                    if front and slot == 3:
                        split(front, 1)
                        split(front, 2)
                    if middle and slot == 6:
                        norm_scale("a1", middle)
                    if last and slot == 6:
                        norm_scale("f1", last)
                    if middle and slot == 7:
                        m = middle
                        pool.wait_ge(x2_done, m.times(1))
                        if m.follows(1):
                            pool.wait_ge(x3_done, m.back(1).times(1))
                        for t in range(TT):
                            ins = pool.tensor_tensor(x2_bc[:, t, :], x2[:, t, :], bias_row[:, BC1, :], ALU.add)
                        ins.then_inc(x2bc_done, 1)
                    if last and slot in (11, 13):
                        l, c = last, (slot - 11) // 2
                        pool.wait_ge(hid_done, l.times(2, c + 1))
                        if l.follows(1):
                            pool.wait_ge(proj_mm, l.back(1).times(1))
                        pool.tensor_tensor(hid2[:, 2 * c:2 * c + 2, :], hid[:, 2 * c:2 * c + 2, :], hid[:, 2 * c:2 * c + 2, :],
                                           ALU.mult).then_inc(hid2_done, 1)
                    if ahead and slot == 12:
                        norm_scale("a0", ahead)

            run_steps(pool, step, {-2: masks})

        @block.scalar
        def _(act):
            def normalise(t, seq, src):
                act.wait_ge(ln_shift[t], seq.times(1))
                if seq.follows(1):
                    act.wait_ge(xn_turned[t], seq.back(1).times(1))
                for i in range(TT):
                    nc.scalar.activation(xn[t][:, i, :], src[:, i, :], ACT.Identity, bias=shift[t][:, i:i + 1],
                                         scale=rstd[t][:, i:i + 1]).then_inc(ln_done[t], 1)

            def copy_turned(t, seq, bank, users):
                act.wait_ge(xn_turned[t], seq.times(1))
                if seq.follows(1):
                    for signal, per in users:
                        act.wait_ge(signal, seq.back(1).times(per))
                nc.scalar.activation(xnT[t][:, :], bank[:, 0:S], ACT.Copy).then_inc(xnT_done[t], 1)

            def step(ahead, front, maxima, heads, middle, last):
                for slot in range(SLOTS + 1):
                    if heads and slot < SLOTS:
                        act.wait_ge(score_mm, heads.times(H, slot + 1))
                        if heads.follows(1) or slot >= PT_RING:
                            act.wait_ge(pv_mm, heads.times(4, (slot - PT_RING) // 4 + 1))
                        nc.scalar.activation(probs[:, slot % PT_RING, :, :].rearrange("p t s -> p (t s)"),
                                             score_bank[slot % 2][:, :], ACT.Exp, scale=SCALE).then_inc(exp_done, 1)
                    if front and slot == 0:
                        copy_turned("a0", front, front_bank, ((qk_mm, 1), (v_mm, 1)))
                    if front and slot == 1:
                        act.wait_ge(qk_mm, front.times(1))
                        if front.follows(1):
                            act.wait_ge(split_done, front.back(1).times(5))
                        for i in range(2):
                            nc.scalar.activation(qk[:, i, :], front_bank[:, i * S:(i + 1) * S], ACT.Identity,
                                                 bias=bias_col[:, i:i + 1]).then_inc(qk_done, 1)
                    if middle and slot == 1:
                        act.wait_ge(y0_turned, middle.times(1))
                        if middle.follows(1):
                            act.wait_ge(wp_mm, middle.back(1).times(1))
                        nc.scalar.activation(yT[:, :], mid_bank[:, 0:S], ACT.Copy).then_inc(yT_done, 1)
                    if middle and slot == 4:
                        normalise("f0", middle, x1)
                    if middle and slot == 5:
                        copy_turned("f0", middle, mid_bank, ((ffn_mm, 1),))
                    if last and slot == 5:
                        act.wait_ge(y1_turned, last.times(1))
                        if last.follows(1):
                            act.wait_ge(wc_mm, last.back(1).times(1))
                        nc.scalar.activation(y1T[:, :], last_bank[:, 0:S], ACT.Copy).then_inc(y1T_done, 1)
                    if middle and slot == 8:
                        normalise("a1", middle, x2)
                    if middle and slot == 9:
                        copy_turned("a1", middle, mid_bank, ((kv1_mm, 1), (q1_mm, 1)))
                    if last and slot == 9:
                        normalise("f1", last, x3)
                    if last and slot == 10:
                        copy_turned("f1", last, last_bank, ((hid_mm, 2),))
                    if last and slot in (11, 13):
                        c = (slot - 11) // 2
                        act.wait_ge(hid_mm, last.times(2, c + 1))
                        if last.follows(1):
                            act.wait_ge(hid2_done, last.back(1).times(2))
                        nc.scalar.activation(hid[:, 2 * c:2 * c + 2, :].rearrange("p c s -> p (c s)"), last_bank[:, :],
                                             ACT.Relu).then_inc(hid_done, 1)
                    if middle and slot == 11:
                        act.wait_ge(k1_min_done, middle.times(1))
                        if middle.follows(1):
                            act.wait_ge(k1_done, middle.back(1).times(1))
                        nc.scalar.activation(k1_exp[:, :, :], k1_min[:, :, :], ACT.Exp).then_inc(k1_exp_done, 1)
                    if middle and slot == 12:
                        act.wait_ge(q1_mm, middle.times(1))
                        if middle.follows(1):
                            act.wait_ge(q1_done, middle.back(1).times(1))
                        nc.scalar.activation(q1[:, :], mid_bank[:, 0:S], ACT.Identity, bias=bias_col[:, 2:3]).then_inc(q1_bias, 1)
                    if middle and slot == 13:
                        act.wait_ge(q1_min_done, middle.times(1))
                        nc.scalar.activation(q1_exp[:, :], q1_min[:, :], ACT.Exp).then_inc(q1_exp_done, 1)
                    if ahead and slot == 14:
                        act.wait_ge(x_in[ahead.ring], ahead.landed(1))
                        normalise("a0", ahead, x_front[:, ahead.ring])
                    if maxima and slot == 15:
                        a, r = maxima, maxima.ring
                        act.wait_ge(max_parts, a.times(2))
                        for half in range(2):
                            for part in range(2):
                                row = half * PAIR_ROWS + NEG_MAX_ROW + part
                                act.dma_start(q_stack[row:row + 1, r, :, :].rearrange("p j (t s) -> p (j t) s", t=TT),
                                              neg_max_parts[16 * half:16 * half + 16, part, :]).then_inc(aug_in[r], 16)
                    if heads and slot == TAIL:
                        act.wait_ge(pv_mm, heads.times(4))
                        if heads.follows(1):
                            act.wait_ge(yraw_turned, heads.back(1).times(1))
                        nc.scalar.activation(yT_raw[:, :, :].rearrange("p b s -> p (b s)"), pv_bank[:, :], ACT.Copy).then_inc(yraw_done, 1)

            run_steps(act, step)

        @block.vector
        def _(dve):
            made = [0]

            def after(ins):
                ins.then_inc(weights_ready, 1)
                made[0] += 1
                dve.wait_ge(weights_ready, made[0])

            nc.vector.memset(v_hat[:, :, :, :, :], 0.0).then_inc(small_made, 1)
            nc.vector.memset(v1_ones[:, :, :], 1.0).then_inc(small_made, 1)
            nc.vector.memset(neg_max[:, :], 0.0).then_inc(small_made, 1)
            dve.wait_ge(small_made, 3)
            for par in range(2):
                vh = v_hat[:, :, :, par::2, 16 * par + DK].rearrange("p r t h -> p (r t) h")
                nc.vector.memset(vh, 1.0).then_inc(small_made, 1)
            dve.wait_ge(small_made, 5)

            def first_weights():
                dve.wait_ge(weight_turned, 1)
                nc.vector.tensor_copy(wT[:, 0:3, :], front_bank[:, 0:3 * P].rearrange("p (a b) -> p a b", a=3)).then_inc(weight_copied, 1)
                nc.vector.memset(zero_rows[:, :], 0.0).then_inc(stacks_ready, 1)
                nc.vector.memset(one_rows[:, :], 1.0).then_inc(stacks_ready, 1)
                nc.vector.memset(q_stack[:, :, :, :].rearrange("p r j s -> p (r j s)").bitcast(F32), 0.0).then_inc(stacks_ready, 1)
                nc.vector.memset(k_stack[:, :, :, :].rearrange("p r h s -> p (r h s)").bitcast(F32), 0.0).then_inc(stacks_ready, 1)
                dve.wait_ge(first_in, 16 * FIRST_DMAS)

            def other_weights():
                dve.wait_ge(weights_in, 16 * WEIGHT_DMAS)
                dve.wait_ge(consts_made, 2)
                for c in range(HC + 1):
                    src = raw_fc[:, c, :] if c < HC else raw_proj[:, :]
                    after(nc.vector.tensor_reduce(row_sum[:, c:c + 1], src, AX.X, ALU.add, apply_absolute_value=True))
                after(nc.vector.tensor_scalar(row_scale[:, 0:HC], row_sum[:, 0:HC], 1.0 / D, MIN_SCALE, ALU.mult, ALU.max))
                after(nc.vector.tensor_scalar(row_scale[:, HC:HC + 1], row_sum[:, HC:HC + 1], 1.0 / HID, MIN_SCALE, ALU.mult, ALU.max))
                after(nc.vector.tensor_scalar(half_scale[:, :], row_scale[:, :], 0.5, None, ALU.mult))
                after(nc.vector.tensor_scalar(neg_half[:, :], row_scale[:, :], -0.5, None, ALU.mult))
                for c in range(HC + 1):
                    src = raw_fc[:, c, :] if c < HC else raw_proj[:, :]
                    w = src.shape[-1]
                    after(nc.vector.tensor_scalar(tern_pos[:, 0:w], src, half_scale[:, c:c + 1], row_scale[:, c:c + 1], ALU.is_gt, ALU.mult))
                    after(nc.vector.tensor_scalar(tern_neg[:, 0:w], src, neg_half[:, c:c + 1], row_scale[:, c:c + 1], ALU.is_lt, ALU.mult))
                    after(nc.vector.tensor_tensor(src, tern_pos[:, 0:w], tern_neg[:, 0:w], ALU.subtract))
                ternary_made[0] = made[0]
                dve.wait_ge(weight_turned, 2)
                nc.vector.tensor_copy(wT[:, 3:7, :], mid_bank[:, :].rearrange("p (a b) -> p a b", a=4)).then_inc(weight_copied, 1)
                dve.wait_ge(weight_turned, 3)
                nc.vector.tensor_copy(wT[:, 7:9, :], last_bank[:, 0:2 * P].rearrange("p (a b) -> p a b", a=2)).then_inc(weight_copied, 1)
                nc.vector.tensor_copy(fbT[:, :], last_bank[:, 2 * P:3 * P]).then_inc(weight_copied, 1)
                dve.wait_ge(weight_turned, 4)
                nc.vector.tensor_copy(uT[:, :], mid_bank[:, :]).then_inc(weight_copied, 1)
                dve.wait_ge(weight_turned, 5)
                nc.vector.tensor_copy(fcT[:, :], last_bank[:, :]).then_inc(weight_copied, 1)
                dve.wait_ge(weight_turned, 6)
                nc.vector.tensor_copy(projT[:, :, :], mid_bank[:, :].rearrange("p (a b) -> p a b", a=HC)).then_inc(weight_copied, 1)
                dve.wait_ge(weight_copied, 7)
                after(nc.vector.tensor_tensor(wT[:, WF, :], wT[:, WF, :], disha2[:, :], ALU.add))
                dve.wait_ge(weight_turned, 7)
                after(nc.vector.tensor_scalar(fbv[:, :], last_bank[0:RK, 0:P], gate_col[:, 0:1], None, ALU.mult))
                fbv_made[0] = made[0]
                dve.wait_ge(weight_turned, 8)
                after(nc.vector.tensor_tensor(fcT[:, :], mid_bank[:, :], fcT[:, :], ALU.add))
                all_made[0] = made[0]

            def norm_stats(t, seq, src):
                if seq.follows(1):
                    dve.wait_ge(ln_mv[t], seq.back(1).times(2))
                for i in range(TT):
                    nc.vector.bn_stats(stats[t][:, i, :], src[:, i, :]).then_inc(ln_stats[t], 1)
                dve.wait_ge(ln_stats[t], seq.times(2))
                if seq.follows(1):
                    dve.wait_ge(ln_pre[t], seq.back(1).times(2))
                hold(dve, dve_passed)
                for i in range(TT):
                    nc.vector.bn_aggr(mv[t][:, i, :], stats[t][:, i, :]).then_inc(ln_mv[t], 1)

            def tile3(ap, b):
                return ap.rearrange("p (t d) -> p t d", t=b)

            def step(ahead, front, maxima, heads, middle, last):
                tile = 0
                for slot in range(SLOTS + 1):
                    if maxima:
                        a = maxima
                        for _ in range(MAX_TILES[slot] if slot < SLOTS else 0):
                            t, j = tile // PAIRS, tile % PAIRS
                            dve.wait_ge(max_mm, a.times(16, tile + 1))
                            if tile == 0 and a.follows(1):
                                dve.wait_ge(max_turned, a.back(1).times(1))
                            dst = neg_max[:, 0:32].rearrange("p (h j t) -> p h j t", h=2, t=TT)[:, :, j, t]
                            nc.vector.tensor_reduce(dst, tile3(max_bank[tile % 2][:, :], 2), AX.X, ALU.max,
                                                    negate=True).then_inc(max_done, 1)
                            tile += 1
                        if slot == 14:
                            dve.wait_ge(max_turned, a.times(1))
                            if a.follows(1):
                                dve.wait_ge(aug_in[a.back(1).ring], a.back(1).landed(AUG_DMAS))
                            nc.vector.tensor_copy(neg_max_parts[:, 0, :], max_bank[1][0:32, 0:P]).then_inc(max_parts, 1)
                            dve.wait_ge(max_parts, a.times(2, 1))
                            nc.vector.tensor_tensor(neg_max_parts[:, 1, :], max_bank[1][0:32, 0:P], neg_max_parts[:, 0, :],
                                                    ALU.subtract).then_inc(max_parts, 1)
                    if last:
                        l = last
                        if slot == 1:
                            dve.wait_ge(state_mm, l.times(1))
                            if l.follows(1):
                                dve.wait_ge(y1_mm, l.back(1).times(1))
                            nc.vector.tensor_tensor(kv_blocks[:, 0:P], last_bank[:, 0:P], block_mask[:, :], ALU.mult).then_inc(state_done, 1)
                            nc.vector.tensor_scalar(kv_blocks[:, P:P + H], head_mask[:, :], last_bank[:, P:P + 1], None, ALU.mult).then_inc(state_done, 1)
                        if slot == 3:
                            dve.wait_ge(y1_mm, l.times(1))
                            if l.follows(1):
                                dve.wait_ge(y1_done, l.back(1).times(1))
                            y1p = tile3(last_bank[:, 0:TT * (P + H)], TT)
                            nc.vector.tensor_scalar(den1[:, :, :], y1p[:, :, P:P + H], Z_EPS, None, ALU.add).then_inc(den1_done, 1)
                            dve.wait_ge(den1_done, l.times(2, 1))
                            nc.vector.reciprocal(inv_den1[:, :, :], den1[:, :, :]).then_inc(den1_done, 1)
                            dve.wait_ge(den1_done, l.times(2, 2))
                            if l.follows(1):
                                dve.wait_ge(y1_turned, l.back(1).times(1))
                            for t in range(TT):
                                ins = nc.vector.tensor_tensor(y1[:, t], y1p[:, t, 0:P].rearrange("p (h d) -> p h d", d=DK),
                                                              inv_den1[:, t, :].unsqueeze(2).broadcast_to([P, H, DK]), ALU.mult)
                            ins.then_inc(y1_done, 1)
                        if slot == 6:
                            dve.wait_ge(wc_mm, l.times(1))
                            dve.wait_ge(x2bc_done, l.times(1))
                            if l.follows(1):
                                dve.wait_ge(x4_done, l.back(1).times(1))
                                dve.wait_ge(ln_done["f1"], l.back(1).times(2))
                            nc.vector.tensor_tensor(x3[:, :, :], tile3(last_bank[:, 0:S], TT), x2_bc[:, :, :], ALU.add).then_inc(x3_done, 1)
                            dve.wait_ge(x3_done, l.times(1))
                            norm_stats("f1", l, x3)
                        if slot == TAIL:
                            dve.wait_ge(proj_mm, l.times(1))
                            if l.follows(RING):
                                dve.wait_ge(out_done[l.ring], l.back(RING).landed(1))
                            nc.vector.tensor_tensor(x4[:, l.ring, :, :], tile3(last_bank[:, 0:S], TT), x3[:, :, :], ALU.add).then_inc(x4_done, 1)
                    if middle:
                        m = middle
                        if slot == 2:
                            dve.wait_ge(wp_mm, m.times(1))
                            dve.wait_ge(xbp_done, m.times(1))
                            if m.follows(1):
                                dve.wait_ge(x2_done, m.back(1).times(1))
                                dve.wait_ge(ln_done["f0"], m.back(1).times(2))
                            nc.vector.tensor_tensor(x1[:, :, :], tile3(mid_bank[:, 0:S], TT), x_bp[:, :, :], ALU.add).then_inc(x1_done, 1)
                            dve.wait_ge(x1_done, m.times(1))
                            norm_stats("f0", m, x1)
                        if slot == 6:
                            dve.wait_ge(ffn_mm, m.times(1))
                            if m.follows(1):
                                dve.wait_ge(ln_done["a1"], m.back(1).times(2))
                                dve.wait_ge(x2bc_done, m.back(1).times(1))
                            nc.vector.tensor_tensor(x2[:, :, :], tile3(mid_bank[:, 0:S], TT), x1[:, :, :], ALU.add).then_inc(x2_done, 1)
                            dve.wait_ge(x2_done, m.times(1))
                            norm_stats("a1", m, x2)
                        if slot == 10:
                            dve.wait_ge(kv1_mm, m.times(1))
                            if m.follows(1):
                                dve.wait_ge(k1_done, m.back(1).times(1))
                                dve.wait_ge(state_mm, m.back(1).times(1))
                            kv = tile3(mid_bank[:, :], TT)
                            nc.vector.tensor_tensor(k1[:, :, :], kv[:, :, 0:P], bias_row[:, BK1:BK1 + 1, :].broadcast_to([P, TT, P]), ALU.add).then_inc(kv1_bias, 1)
                            nc.vector.tensor_tensor(v1_ones[:, :, 0:P], kv[:, :, P:2 * P], bias_row[:, BV1:BV1 + 1, :].broadcast_to([P, TT, P]), ALU.add).then_inc(kv1_bias, 1)
                            dve.wait_ge(kv1_bias, m.times(2, 1))
                            if m.follows(1):
                                dve.wait_ge(k1_exp_done, m.back(1).times(1))
                            nc.vector.tensor_scalar(k1_min[:, :, :], k1[:, :, :], 0.0, None, ALU.min).then_inc(k1_min_done, 1)
                        if slot == 12:
                            dve.wait_ge(k1_exp_done, m.times(1))
                            if m.follows(1):
                                dve.wait_ge(state_mm, m.back(1).times(1))
                            nc.vector.scalar_tensor_tensor(k1_elu[:, :, :], k1[:, :, :], 0.0, k1_exp[:, :, :], ALU.max, ALU.add).then_inc(k1_done, 1)
                            dve.wait_ge(q1_bias, m.times(1))
                            if m.follows(1):
                                dve.wait_ge(q1_exp_done, m.back(1).times(1))
                            nc.vector.tensor_scalar(q1_min[:, :], q1[:, :], 0.0, None, ALU.min).then_inc(q1_min_done, 1)
                        if slot == 14:
                            dve.wait_ge(q1_exp_done, m.times(1))
                            if m.follows(1):
                                dve.wait_ge(y1_mm, m.back(1).times(1))
                            nc.vector.scalar_tensor_tensor(q1_elu[:, :], q1[:, :], 0.0, q1_exp[:, :], ALU.max, ALU.add).then_inc(q1_done, 1)
                    if front and slot == 3:
                        f = front
                        dve.wait_ge(v_mm, f.times(1))
                        if f.follows(RING):
                            dve.wait_ge(pv_mm, f.back(RING).times(4))
                        for par in range(2):
                            dst = v_hat[:, f.ring, :, par::2, 16 * par:16 * par + DK]
                            src = front_bank[:, 0:S].rearrange("p (t h a d) -> p t h a d", t=TT, a=2, d=DK)[:, :, :, par, :]
                            b = bias_row[:, BV:BV + 1, :].rearrange("p o (h a d) -> p o h a d", a=2, d=DK)[:, :, :, par, :]
                            nc.vector.tensor_tensor(dst, src, b.broadcast_to([P, TT, PAIRS, DK]), ALU.add).then_inc(v_done, 1)
                    if ahead and slot == 12:
                        dve.wait_ge(x_in[ahead.ring], ahead.landed(1))
                        norm_stats("a0", ahead, x_front[:, ahead.ring])
                    if heads and slot == TAIL:
                        h = heads
                        dve.wait_ge(yraw_turned, h.times(1))
                        if h.follows(1):
                            dve.wait_ge(y0_turned, h.back(1).times(1))
                        heads_view = max_bank[0][:, :].rearrange("p (n c) -> p n c", c=16)
                        nc.vector.reciprocal(inv_den[:, :], heads_view[:, :, DK]).then_inc(den_done, 1)
                        dve.wait_ge(den_done, h.times(1))
                        nc.vector.tensor_tensor(y0[:, :, :], heads_view[:, :, 0:DK],
                                                inv_den[:, :].unsqueeze(2).broadcast_to([P, TT * H, DK]), ALU.mult).then_inc(y0_done, 1)

            run_steps(dve, step, {-2: first_weights, -1: other_weights})

        @block.tensor
        def _(pe):
            def turn_all(bank, srcs):
                for i, s in enumerate(srcs):
                    ins = nc.tensor.transpose(bank[:, i * P:(i + 1) * P], s, ident[:, :])
                ins.then_inc(weight_turned, 1)

            def first_weights():
                pe.wait_ge(ident_made, 1)
                pe.wait_ge(first_in, 16 * FIRST_DMAS)
                turn_all(front_bank, [raw[:, i, :] for i in (WQ, WK, WV)])
                pe.wait_ge(weight_copied, 1)

            def other_weights():
                pe.wait_ge(weights_in, 16 * WEIGHT_DMAS)
                turn_all(mid_bank, [raw[:, i, :] for i in range(3, 7)])
                turn_all(last_bank, [raw[:, 7, :], raw[:, 8, :], raw_fb[:, :]])
                pe.wait_ge(weight_copied, 2)
                turn_all(mid_bank, [raw_u[:, c, :] for c in range(HC)])
                pe.wait_ge(weight_copied, 4)
                pe.wait_ge(weights_ready, ternary_made[0])
                turn_all(last_bank, [raw_fc[:, c, :] for c in range(HC)])
                pe.wait_ge(weight_copied, 5)
                turn_all(mid_bank, [raw_proj[:, c * P:(c + 1) * P] for c in range(HC)])
                pe.wait_ge(weight_copied, 6)
                nc.tensor.matmul(last_bank[0:RK, 0:P], fbT[0:RK, 0:RK], raw_v[:, :], start=True, stop=True).then_inc(weight_turned, 1)
                pe.wait_ge(weight_copied, 7)
                pe.wait_ge(weights_ready, fbv_made[0])
                nc.tensor.matmul(mid_bank[:, :], fbv[:, :], uT[0:RK, :], start=True, stop=True).then_inc(weight_turned, 1)
                pe.wait_ge(ones_in, 32)

            def all_weights():
                pe.wait_ge(weights_ready, all_made[0])

            def turn_tokens(bank, src, signal):
                for t in range(TT):
                    ins = nc.tensor.transpose(bank[:, t * P:(t + 1) * P], src(t), ident[:, :])
                ins.then_inc(signal, 1)

            def by_token(bank, lhs, w, signal, width=P):
                for t in range(TT):
                    ins = nc.tensor.matmul(bank[:, t * width:(t + 1) * width], lhs[:, t * P:(t + 1) * P], w, start=True, stop=True)
                ins.then_inc(signal, 1)

            def pv(heads, g):
                v, b, a = heads.ring, g // 2, g % 2
                pe.wait_ge(exp_done, heads.times(H, 4 * g + 4))
                if g == 0 and heads.follows(1):
                    pe.wait_ge(yraw_done, heads.back(1).times(1))
                for t in range(TT):
                    for j in range(4):
                        h = 8 * b + 2 * j + a
                        ins = nc.tensor.matmul(pv_bank[32 * j:32 * j + 32, b * S:(b + 1) * S], v_hat[:, v, t, h, :],
                                               probs[:, (4 * g + j) % PT_RING, t, :], start=(a == 0 and t == 0),
                                               stop=(a == 1 and t == TT - 1))
                ins.then_inc(pv_mm, 1)

            def project(l, t):
                for c in range(HC):
                    ins = nc.tensor.matmul(last_bank[:, t * P:(t + 1) * P], hid2[:, c, t * P:(t + 1) * P],
                                           projT[:, c, :], start=(c == 0), stop=(c == HC - 1))
                return ins

            def step(ahead, front, maxima, heads, middle, last):
                tile = 0
                for slot in range(SLOTS):
                    if heads:
                        r = heads.ring
                        h = 8 * (slot // 8) + 2 * (slot % 4) + slot // 4 % 2
                        if slot == 0:
                            pe.wait_ge(aug_in[r], heads.landed(AUG_DMAS))
                        if heads.follows(1) or slot >= 2:
                            pe.wait_ge(exp_done, heads.times(H, slot - 1))
                        for t in range(TT):
                            ins = nc.tensor.matmul(score_bank[slot % 2][:, t * S:(t + 1) * S], k_stack[:, r, h, t * P:(t + 1) * P],
                                                   q_stack[:, r, h // 2, :], start=True, stop=True)
                        ins.then_inc(score_mm, 1)
                    if maxima:
                        a, r = maxima, maxima.ring
                        for _ in range(MAX_TILES[slot]):
                            t, j = tile // PAIRS, tile % PAIRS
                            if tile == 0:
                                pe.wait_ge(stack_in[r], a.landed(STACK_DMAS))
                                if a.follows(2):
                                    pe.wait_ge(y0_done, a.back(2).times(1))
                            if tile == 1 and a.follows(1):
                                pe.wait_ge(max_parts, a.back(1).times(2))
                            if tile >= 2:
                                pe.wait_ge(max_done, a.times(16, tile - 1))
                            nc.tensor.matmul(max_bank[tile % 2][:, :], q_stack[:, r, j, t * P:(t + 1) * P],
                                             k_stack[:, r, 2 * j:2 * j + 2, :].rearrange("p h s -> p (h s)"), start=True, stop=True).then_inc(max_mm, 1)
                            tile += 1
                        if slot == 14:
                            pe.wait_ge(max_done, a.times(16))
                            nc.tensor.transpose(max_bank[1][:, 0:P], neg_max[:, :], ident[:, :]).then_inc(max_turned, 1)
                    if heads and slot >= 5 and slot % 4 == 1:
                        pv(heads, slot // 4 - 1)
                    if last:
                        l = last
                        if slot == 1:
                            pe.wait_ge(k1_done, l.times(1))
                            if l.follows(1):
                                pe.wait_ge(x4_done, l.back(1).times(1))
                            for t in range(TT):
                                ins = nc.tensor.matmul(last_bank[:, 0:P + 1], k1_elu[:, t, :], v1_ones[:, t, :], start=(t == 0), stop=(t == TT - 1))
                            ins.then_inc(state_mm, 1)
                        if slot == 3:
                            pe.wait_ge(state_done, l.times(2))
                            pe.wait_ge(q1_done, l.times(1))
                            by_token(last_bank, q1_elu, kv_blocks[:, :], y1_mm, P + H)
                        if slot == 5:
                            pe.wait_ge(y1_done, l.times(1))
                            turn_tokens(last_bank, lambda t: y1[:, t].rearrange("p h d -> p (h d)"), y1_turned)
                        if slot == 6:
                            pe.wait_ge(y1T_done, l.times(1))
                            by_token(last_bank, y1T, wT[:, WC1, :], wc_mm)
                        if slot == 10:
                            pe.wait_ge(ln_done["f1"], l.times(2))
                            turn_tokens(last_bank, lambda t: xn["f1"][:, t, :], xn_turned["f1"])
                        if slot in (11, 13):
                            pe.wait_ge(xnT_done["f1"], l.times(1))
                            if slot == 13:
                                pe.wait_ge(hid_done, l.times(2, 1))
                            for i in range(2):
                                c = slot - 11 + i
                                ins = nc.tensor.matmul(last_bank[:, i * S:(i + 1) * S], fcT[:, c * P:(c + 1) * P], xnT["f1"][:, :],
                                                       start=True, stop=True)
                            ins.then_inc(hid_mm, 1)
                    if middle:
                        m = middle
                        if slot == 1:
                            pe.wait_ge(y0_done, m.times(1))
                            if m.follows(1):
                                pe.wait_ge(q1_bias, m.back(1).times(1))
                            turn_tokens(mid_bank, lambda t: y0[:, t * H:(t + 1) * H, :].rearrange("p h d -> p (h d)"), y0_turned)
                        if slot == 2:
                            pe.wait_ge(yT_done, m.times(1))
                            by_token(mid_bank, yT, wT[:, WP_, :], wp_mm)
                        if slot == 5:
                            pe.wait_ge(ln_done["f0"], m.times(2))
                            turn_tokens(mid_bank, lambda t: xn["f0"][:, t, :], xn_turned["f0"])
                        if slot == 6:
                            pe.wait_ge(xnT_done["f0"], m.times(1))
                            by_token(mid_bank, xnT["f0"], wT[:, WF, :], ffn_mm)
                        if slot == 9:
                            pe.wait_ge(ln_done["a1"], m.times(2))
                            turn_tokens(mid_bank, lambda t: xn["a1"][:, t, :], xn_turned["a1"])
                        if slot == 10:
                            pe.wait_ge(xnT_done["a1"], m.times(1))
                            by_token(mid_bank, xnT["a1"], wT[:, WK1:WV1 + 1, :].rearrange("p a b -> p (a b)"), kv1_mm, 2 * P)
                        if slot == 12:
                            pe.wait_ge(kv1_bias, m.times(2))
                            nc.tensor.matmul(mid_bank[:, 0:S], wT[:, WQ1, :], xnT["a1"][:, :], start=True, stop=True).then_inc(q1_mm, 1)
                    if front:
                        f = front
                        if slot == 0:
                            pe.wait_ge(ln_done["a0"], f.times(2))
                            if f.follows(1):
                                pe.wait_ge(v_done, f.back(1).times(2))
                            turn_tokens(front_bank, lambda t: xn["a0"][:, t, :], xn_turned["a0"])
                        if slot == 1:
                            pe.wait_ge(xnT_done["a0"], f.times(1))
                            for i, w in enumerate((WQ, WK)):
                                ins = nc.tensor.matmul(front_bank[:, i * S:(i + 1) * S], wT[:, w, :], xnT["a0"][:, :], start=True, stop=True)
                            ins.then_inc(qk_mm, 1)
                        if slot == 3:
                            pe.wait_ge(qk_done, f.times(2))
                            by_token(front_bank, xnT["a0"], wT[:, WV, :], v_mm)
                if last:
                    pe.wait_ge(hid_done, last.times(2))
                    pe.wait_ge(hid2_done, last.times(2))
                    project(last, 0)
                if heads:
                    pv(heads, 3)
                if last:
                    project(last, 1).then_inc(proj_mm, 1)
                if heads:
                    pe.wait_ge(yraw_done, heads.times(1))
                    if heads.follows(1):
                        pe.wait_ge(y0_done, heads.back(1).times(1))
                    for t in range(TT):
                        for b in range(2):
                            ins = nc.tensor.transpose(max_bank[0][:, (2 * t + b) * P:(2 * t + b + 1) * P],
                                                      yT_raw[:, b, t * P:(t + 1) * P], ident[:, :])
                    ins.then_inc(yraw_turned, 1)

            run_steps(pe, step, {-2: first_weights, -1: other_weights, 1: all_weights})


_INS = ['L0_attn_x', 'L0_attn_Wq', 'L0_attn_bq', 'L0_attn_Wk', 'L0_attn_bk', 'L0_attn_Wv', 'L0_attn_bv',
        'L0_attn_Wp', 'L0_attn_bp', 'L0_ffn_weight', 'L0_ffn_disha', 'L1_attn_Wq', 'L1_attn_bq', 'L1_attn_Wk',
        'L1_attn_bk', 'L1_attn_Wv', 'L1_attn_bv', 'L1_attn_Wc', 'L1_attn_bc', 'L1_ffn_fast_b', 'L1_ffn_w_fc',
        'L1_ffn_w_proj', 'L1_ffn_u', 'L1_ffn_v', 'L1_ffn_gate']


def kernel(**inputs):
    import numpy as _np
    import concourse.bacc as _bacc
    from concourse import mybir as _mybir
    from concourse.bass_utils import run_bass_kernel_spmd as _run

    nc = _bacc.Bacc("TRN2", target_bir_lowering=False, num_devices=1)
    arrays, args = {}, []
    for name in _INS:
        a = _np.ascontiguousarray(inputs[name])
        if a.ndim == 0:
            a = a.reshape(1)
        arrays[f"in_{name}_dram"] = a
        args.append(nc.dram_tensor(f"in_{name}_dram", a.shape, _mybir.dt.from_np(a.dtype), kind="ExternalInput").ap())
    shape = arrays["in_L0_attn_x_dram"].shape
    args.append(nc.dram_tensor("out_0_dram", shape, _mybir.dt.float32, kind="ExternalOutput").ap())
    two_layer_kernel(nc, *args)
    r = _run(nc, [arrays], core_ids=[0])
    return r.results[0]["out_0_dram"]
```

```python
from contextlib import ExitStack

import concourse.bass as bass
from concourse import mybir

F32 = mybir.dt.float32
BF16 = mybir.dt.bfloat16
ALU = mybir.AluOpType
ACT = mybir.ActivationFunctionType
AX = mybir.AxisListType

P = 128
EPS = 1e-5
Z_EPS = 1e-6
MIN_SCALE = 1e-5
RING = 3
PAIR_ROWS = 64
NEG_MAX_ROW = 48
RUNS = [(3, 0, 0), (2, 0, 1), (1, 0, 2)]
PARTS_DMAS = 3 * 2
STACK_DMAS = 2 * 2 * len(RUNS) + 2
AUG_DMAS = 4
SLOTS = 16
LEAD, TRAIL = 3, 3
MAX_TILES = [2, 2, 1, 0, 1, 2, 2, 0, 2, 0, 2, 1, 1, 0, 0, 0]
PT_RING = 8


class Seq:

    def __init__(self, const, turn=None):
        self.const, self.turn = const, turn
        self.ring = const % RING
        self.n = const if turn is None else turn * RING + const
        self.round = const // RING if turn is None else turn + const // RING

    def back(self, k):
        return Seq(self.const - k, self.turn)

    def follows(self, k):
        return self.turn is not None or self.const >= k

    def times(self, per, count=None):
        return self.n * per + (per if count is None else count)

    def landed(self, per):
        return (self.round + 1) * (16 * per)


def two_layer_kernel(nc, x, Wq, bq, Wk, bk, Wv, bv, Wp, bp, ffn_w, disha,
                     Wq1, bq1, Wk1, bk1, Wv1, bv1, Wc1, bc1, fast_b, w_fc, w_proj, u_fc, v_fc, gate, out):
    N, S, D = x.shape
    H, DK = 16, 8
    TT = S // P
    HID = w_fc.shape[0]
    HC = HID // P
    RK = fast_b.shape[0]
    RD = disha.shape[0]
    SCALE = 1.0 / DK ** 0.5
    PAIRS = H // 2
    assert D == P and TT == 2 and H * DK == D

    x_t = x.rearrange("n (t p) d -> n p t d", p=P)
    out_t = out.rearrange("n (t p) d -> n p t d", p=P)
    parts_dram = nc.dram_tensor("qk_parts", (RING, PAIRS, 2, 2, 3, DK, S), BF16, kind="Internal").ap()

    ctx = ExitStack()
    with ctx:
        def sb(name, shape, dt=F32):
            return ctx.enter_context(nc.sbuf_tensor(name, shape, dt))

        def psum(name):
            return ctx.enter_context(nc.psum_tensor(name, [P, 512], F32))

        def sem(name):
            return ctx.enter_context(nc.semaphore(name))

        ident = sb("ident", [P, P])
        ones_col = sb("ones_col", [P, 1])
        half_pow = sb("half_pow", [P, TT])
        head_mask = sb("head_mask", [P, H])
        block_mask = sb("block_mask", [P, P])
        zero_row = sb("zero_row", [2, 1, S], BF16)
        one_row = sb("one_row", [2, 1, S], BF16)
        raw = sb("raw", [P, 9, P])
        raw_fc = sb("raw_fc", [P, HC, P])
        raw_proj = sb("raw_proj", [P, HID])
        raw_u = sb("raw_u", [P, HC, P])
        raw_fb = sb("raw_fb", [P, P])
        raw_v = sb("raw_v", [RK, P])
        disha2 = sb("disha2", [P, P])
        wT = sb("wT", [P, 9, P])
        fcT = sb("fcT", [P, HID])
        projT = sb("projT", [P, HC, P])
        uT = sb("uT", [P, HID])
        fbT = sb("fbT", [P, P])
        fbv = sb("fbv", [RK, P])
        gate_col = sb("gate_col", [RK, 1])
        tern_pos = sb("tern_pos", [P, HID])
        tern_neg = sb("tern_neg", [P, HID])
        row_sum = sb("row_sum", [P, HC + 1])
        row_scale = sb("row_scale", [P, HC + 1])
        half_scale = sb("half_scale", [P, HC + 1])
        neg_half = sb("neg_half", [P, HC + 1])
        bias_col = sb("bias_col", [P, 3])
        bias_row = sb("bias_row", [P, 5, P])

        x_front = sb("x_front", [P, RING, TT, P])
        xn = {t: sb(f"xn_{t}", [P, TT, P]) for t in ("a0", "f0", "a1", "f1")}
        xnT = {t: sb(f"xnT_{t}", [P, S]) for t in ("a0", "f0", "a1", "f1")}
        stats = {t: sb(f"stats_{t}", [P, TT, 6]) for t in xn}
        mv = {t: sb(f"mv_{t}", [P, TT, 2]) for t in xn}
        var_eps = {t: sb(f"var_eps_{t}", [P, TT]) for t in xn}
        neg_mean = {t: sb(f"neg_mean_{t}", [P, TT]) for t in xn}
        rstd = {t: sb(f"rstd_{t}", [P, TT]) for t in xn}
        shift = {t: sb(f"shift_{t}", [P, TT]) for t in xn}
        qk = sb("qk", [P, 2, S])
        rest = [sb(f"rest{i}", [P, 2, S]) for i in range(2)]
        parts = sb("parts", [P, RING, 3, 2, S], BF16)
        q_stack = sb("q_stack", [P, RING, PAIRS, S], BF16)
        k_stack = sb("k_stack", [P, RING, H, S], BF16)
        v_hat = sb("v_hat", [P, RING, TT, H, 32])
        neg_max = sb("neg_max", [P, P])
        neg_max_parts = sb("neg_max_parts", [32, 2, P], BF16)
        probs = sb("probs", [P, PT_RING, TT, S])
        yT_raw = sb("yT_raw", [P, 2, S])
        inv_den = sb("inv_den", [P, TT * H])
        y0 = sb("y0", [P, TT * H, DK])
        x_mid = sb("x_mid", [P, RING, TT, P])
        x_bp = sb("x_bp", [P, TT, P])
        yT = sb("yT", [P, S])
        x1 = sb("x1", [P, TT, P])
        x2 = sb("x2", [P, TT, P])
        x2_bc = sb("x2_bc", [P, TT, P])
        q1 = sb("q1", [P, S])
        q1_min = sb("q1_min", [P, S])
        q1_exp = sb("q1_exp", [P, S])
        q1_elu = sb("q1_elu", [P, S])
        k1 = sb("k1", [P, TT, P])
        k1_min = sb("k1_min", [P, TT, P])
        k1_exp = sb("k1_exp", [P, TT, P])
        k1_elu = sb("k1_elu", [P, TT, P])
        v1_ones = sb("v1_ones", [P, TT, P + 1])
        kv_blocks = sb("kv_blocks", [P, P + H])
        den1 = sb("den1", [P, TT, H])
        inv_den1 = sb("inv_den1", [P, TT, H])
        y1 = sb("y1", [P, TT, H, DK])
        y1T = sb("y1T", [P, S])
        x3 = sb("x3", [P, TT, P])
        hid = sb("hid", [P, HC, S])
        hid2 = sb("hid2", [P, HC, S])
        x4 = sb("x4", [P, TT, P])

        max_bank = [psum(f"max_bank{i}") for i in range(2)]
        score_bank = [psum(f"score_bank{i}") for i in range(2)]
        pv_bank = psum("pv_bank")
        front_bank = psum("front_bank")
        mid_bank = psum("mid_bank")
        last_bank = psum("last_bank")

        first_in = sem("first_in")
        weights_in = sem("weights_in")
        ones_in = sem("ones_in")
        small_made = sem("small_made")
        pads_zero = sem("pads_zero")
        ident_made = sem("ident_made")
        consts_made = sem("consts_made")
        stacks_ready = sem("stacks_ready")
        prep_chain = sem("prep_chain")
        weight_turned = sem("weight_turned")
        weight_copied = sem("weight_copied")
        weights_ready = sem("weights_ready")
        x_in = [sem(f"x_in{r}") for r in range(RING)]
        x_mid_in = [sem(f"x_mid_in{r}") for r in range(RING)]
        parts_out = [sem(f"parts_out{r}") for r in range(RING)]
        stack_in = [sem(f"stack_in{r}") for r in range(RING)]
        aug_in = [sem(f"aug_in{r}") for r in range(RING)]
        out_done = [sem(f"out_done{r}") for r in range(RING)]
        ln_stats = {t: sem(f"ln_stats_{t}") for t in xn}
        ln_mv = {t: sem(f"ln_mv_{t}") for t in xn}
        ln_pre = {t: sem(f"ln_pre_{t}") for t in xn}
        ln_rstd = {t: sem(f"ln_rstd_{t}") for t in xn}
        ln_shift = {t: sem(f"ln_shift_{t}") for t in xn}
        ln_done = {t: sem(f"ln_done_{t}") for t in xn}
        xn_turned = {t: sem(f"xn_turned_{t}") for t in xn}
        xnT_done = {t: sem(f"xnT_done_{t}") for t in xn}
        qk_mm = sem("qk_mm")
        qk_done = sem("qk_done")
        v_mm = sem("v_mm")
        v_done = sem("v_done")
        split_done = sem("split_done")
        max_mm = sem("max_mm")
        max_done = sem("max_done")
        max_turned = sem("max_turned")
        max_parts = sem("max_parts")
        score_mm = sem("score_mm")
        exp_done = sem("exp_done")
        pv_mm = sem("pv_mm")
        yraw_done = sem("yraw_done")
        yraw_turned = sem("yraw_turned")
        den_done = sem("den_done")
        y0_done = sem("y0_done")
        y0_turned = sem("y0_turned")
        yT_done = sem("yT_done")
        xbp_done = sem("xbp_done")
        wp_mm = sem("wp_mm")
        x1_done = sem("x1_done")
        ffn_mm = sem("ffn_mm")
        x2_done = sem("x2_done")
        x2bc_done = sem("x2bc_done")
        kv1_mm = sem("kv1_mm")
        kv1_bias = sem("kv1_bias")
        q1_mm = sem("q1_mm")
        q1_bias = sem("q1_bias")
        q1_min_done = sem("q1_min_done")
        q1_exp_done = sem("q1_exp_done")
        q1_done = sem("q1_done")
        k1_min_done = sem("k1_min_done")
        k1_exp_done = sem("k1_exp_done")
        k1_done = sem("k1_done")
        state_mm = sem("state_mm")
        state_done = sem("state_done")
        y1_mm = sem("y1_mm")
        den1_done = sem("den1_done")
        y1_done = sem("y1_done")
        y1_turned = sem("y1_turned")
        y1T_done = sem("y1T_done")
        wc_mm = sem("wc_mm")
        x3_done = sem("x3_done")
        hid_mm = sem("hid_mm")
        hid_done = sem("hid_done")
        hid2_done = sem("hid2_done")
        proj_mm = sem("proj_mm")
        x4_done = sem("x4_done")
        dve_passed, pool_passed, sp_passed = sem("dve_passed"), sem("pool_passed"), sem("sp_passed")

        ternary_made, fbv_made, all_made = [0], [0], [0]

        block = ctx.enter_context(nc.Block())

        WQ, WK, WV, WP_, WF, WQ1, WK1, WV1, WC1 = range(9)
        square = [Wq, Wk, Wv, Wp, ffn_w, Wq1, Wk1, Wv1, Wc1]
        BV, BP, BK1, BV1, BC1 = range(5)
        FIRST_DMAS = 3 + 2 + 1
        WEIGHT_DMAS = 6 + 2 + 1 + 1 + 1 + 2 + 1 + 1 + 4

        def hold(eng, passed):
            eng.sem_inc(passed, 1)

        def run_steps(eng, step, before={}):
            def go(const, turn=None):
                def stage(off):
                    c = const + off
                    return Seq(c, turn) if turn is not None or 0 <= c < N else None
                step(stage(LEAD), stage(2), stage(1), stage(0), stage(-1), stage(-2), stage(-TRAIL))
            loop_from = TRAIL + 1
            turns = (N - LEAD - loop_from) // RING
            for s in range(-LEAD, loop_from):
                if s in before:
                    before[s]()
                go(s)
            with eng.Fori(0, turns) as turn:
                for k in range(RING):
                    go(loop_from + k, turn)
            for s in range(loop_from + turns * RING, N + TRAIL):
                go(s)

        @block.sync
        def _(sp):
            sp.dma_start(x_front[:, 0, :, :], x_t[0]).then_inc(x_in[0], 16)
            for i in (WQ, WK, WV):
                sp.dma_start(raw[:, i, :], square[i]).then_inc(first_in, 16)
            for i, b in enumerate((bq, bk)):
                sp.dma_start(bias_col[:, i:i + 1], b.rearrange("(p a) -> p a", a=1)).then_inc(first_in, 16)
            sp.dma_start(bias_row[:, BV, :], bv.partition_broadcast(P)).then_inc(first_in, 16)
            for n in range(1, RING):
                sp.dma_start(x_front[:, n, :, :], x_t[n]).then_inc(x_in[n], 16)
            for i in range(WP_, WC1 + 1):
                sp.dma_start(raw[:, i, :], square[i]).then_inc(weights_in, 16)
            sp.dma_start(raw_fc[:, :, :], w_fc.rearrange("(c p) d -> p c d", p=P)).then_inc(weights_in, 16)
            sp.dma_start(raw_proj[:, :], w_proj).then_inc(weights_in, 16)
            sp.wait_ge(pads_zero, 2)
            sp.dma_start(raw_u[:, :, 0:RK], u_fc.rearrange("(c p) r -> p c r", p=P)).then_inc(weights_in, 16)
            sp.dma_start(raw_fb[0:RK, 0:RK], fast_b).then_inc(weights_in, 16)
            sp.dma_start(raw_v[:, :], v_fc).then_inc(weights_in, 16)
            for i in range(P // RD):
                sp.dma_start(disha2[i * RD:(i + 1) * RD, :], disha).then_inc(weights_in, 16)
            sp.dma_start(gate_col[:, :], gate.partition_broadcast(RK)).then_inc(weights_in, 16)
            sp.dma_start(bias_col[:, 2:3], bq1.rearrange("(p a) -> p a", a=1)).then_inc(weights_in, 16)
            for i, b in ((BP, bp), (BK1, bk1), (BV1, bv1), (BC1, bc1)):
                sp.dma_start(bias_row[:, i, :], b.partition_broadcast(P)).then_inc(weights_in, 16)

            def rows_of_ones():
                sp.wait_ge(stacks_ready, 4)
                for half in range(2):
                    row = half * PAIR_ROWS + NEG_MAX_ROW
                    sp.dma_start(k_stack[row:row + 2, :, half::2, :].rearrange("p r j s -> p (r j) s"),
                                 one_row[:, :, :].broadcast_to([2, RING * PAIRS, S])).then_inc(ones_in, 16)

            def step(ahead, front, maxima, heads, middle, linear, last):
                if ahead and ahead.follows(RING):
                    sp.wait_ge(ln_done["a0"], ahead.back(RING).times(2))
                    sp.wait_ge(ln_stats["a0"], ahead.back(RING).times(2))
                    hold(sp, sp_passed)
                    sp.dma_start(x_front[:, ahead.ring, :, :], x_t[ahead.n]).then_inc(x_in[ahead.ring], 16)
                if heads:
                    if heads.follows(RING):
                        sp.wait_ge(xbp_done, heads.back(RING).times(1))
                        hold(sp, sp_passed)
                    sp.dma_start(x_mid[:, heads.ring, :, :], x_t[heads.n]).then_inc(x_mid_in[heads.ring], 16)
                if front:
                    f, r = front, front.ring
                    if f.follows(RING):
                        sp.wait_ge(stack_in[r], f.back(RING).landed(STACK_DMAS))
                        sp.wait_ge(score_mm, f.back(RING).times(H))
                        hold(sp, sp_passed)
                    for half in range(2):
                        row = half * PAIR_ROWS + NEG_MAX_ROW
                        sp.dma_start(q_stack[row:row + 2, r, :, :],
                                     zero_row[:, :, :].broadcast_to([2, PAIRS, S])).then_inc(stack_in[r], 16)
                    for part in range(3):
                        sp.wait_ge(split_done, f.times(5, (1, 3, 5)[part]))
                        hold(sp, sp_passed)
                        for a in range(2):
                            place = part if a == 0 else 2 - part
                            sp.dma_start(parts_dram[r, :, :, a, place].rearrange("j h d s -> (j h) d s"),
                                         parts[:, r, part, a, :]).then_inc(parts_out[r], 16)
                    sp.wait_ge(parts_out[r], f.landed(PARTS_DMAS))
                    for half in range(2):
                        row = half * PAIR_ROWS
                        for run, q_place, k_place in RUNS:
                            end = row + run * DK
                            sp.dma_start(q_stack[row:end, r, :, :],
                                         parts_dram[r, :, half, 0, q_place:q_place + run].rearrange("j n d s -> (n d) j s")).then_inc(stack_in[r], 16)
                            sp.dma_start(k_stack[row:end, r, half::2, :],
                                         parts_dram[r, :, half, 1, k_place:k_place + run].rearrange("j n d s -> (n d) j s")).then_inc(stack_in[r], 16)
                            row = end
                if maxima:
                    a, r = maxima, maxima.ring
                    sp.wait_ge(max_parts, a.times(2))
                    hold(sp, sp_passed)
                    for half in range(2):
                        for part in range(2):
                            row = half * PAIR_ROWS + NEG_MAX_ROW + part
                            sp.dma_start(q_stack[row:row + 1, r, :, :].rearrange("p j (t s) -> p (j t) s", t=TT),
                                         neg_max_parts[16 * half:16 * half + 16, part, :]).then_inc(aug_in[r], 16)
                if last:
                    sp.wait_ge(x4_done, last.times(1))
                    hold(sp, sp_passed)
                    sp.dma_start(out_t[last.n], x4[:, :, :]).then_inc(out_done[last.ring], 16)

            run_steps(sp, step, {-2: rows_of_ones})
            for n in range(N - RING, N):
                sp.wait_ge(out_done[Seq(n).ring], Seq(n).landed(1))

        @block.gpsimd
        def _(pool):
            pool.memset(ident[:, :], 0.0).then_inc(prep_chain, 1)
            pool.memset(half_pow[:, :], -0.5).then_inc(prep_chain, 1)
            pool.wait_ge(prep_chain, 2)
            pool.affine_select(out=ident[:, :], in_=ident[:, :], compare_op=ALU.not_equal, fill=1.0, base=0,
                               pattern=[[-1, P]], channel_multiplier=1).then_inc(ident_made, 1)
            pool.memset(raw_u[:, :, :], 0.0).then_inc(pads_zero, 1)
            pool.memset(raw_fb[:, :], 0.0).then_inc(pads_zero, 1)
            pool.memset(q_stack[:, :, :, :].rearrange("p r j s -> p (r j s)").bitcast(F32), 0.0).then_inc(stacks_ready, 1)
            pool.memset(zero_row[:, :, :], 0.0).then_inc(stacks_ready, 1)
            pool.memset(one_row[:, :, :], 1.0).then_inc(stacks_ready, 1)

            def masks():
                pool.memset(block_mask[:, :], 1.0).then_inc(prep_chain, 1)
                pool.memset(head_mask[:, :], 1.0).then_inc(prep_chain, 1)
                pool.wait_ge(prep_chain, 4)
                bm = block_mask[:, :].rearrange("p (h e) -> p h e", e=DK)
                pool.affine_select(out=bm, in_=bm, compare_op=ALU.is_ge, fill=0.0, base=0,
                                   pattern=[[-DK, H], [0, DK]], channel_multiplier=1).then_inc(prep_chain, 1)
                pool.affine_select(out=head_mask[:, :], in_=head_mask[:, :], compare_op=ALU.is_ge, fill=0.0, base=0,
                                   pattern=[[-DK, H]], channel_multiplier=1).then_inc(prep_chain, 1)
                pool.wait_ge(prep_chain, 6)
                pool.affine_select(out=bm, in_=bm, compare_op=ALU.is_ge, fill=0.0, base=DK - 1,
                                   pattern=[[DK, H], [0, DK]], channel_multiplier=-1).then_inc(consts_made, 1)
                pool.affine_select(out=head_mask[:, :], in_=head_mask[:, :], compare_op=ALU.is_ge, fill=0.0, base=DK - 1,
                                   pattern=[[DK, H]], channel_multiplier=-1).then_inc(consts_made, 1)

            def biases():
                pool.wait_ge(weights_in, 16 * WEIGHT_DMAS)

            def norm_scale(t, seq):
                pool.wait_ge(ln_mv[t], seq.times(2))
                if seq.follows(1):
                    pool.wait_ge(ln_done[t], seq.back(1).times(2))
                hold(pool, pool_passed)
                pool.tensor_scalar(var_eps[t][:, :], mv[t][:, :, 1], EPS, 1.0, ALU.add, ALU.mult).then_inc(ln_pre[t], 1)
                pool.tensor_scalar(neg_mean[t][:, :], mv[t][:, :, 0], -1.0, 1.0, ALU.mult, ALU.mult).then_inc(ln_pre[t], 1)
                pool.wait_ge(ln_pre[t], seq.times(2))
                pool.tensor_tensor(rstd[t][:, :], var_eps[t][:, :], half_pow[:, :], ALU.pow).then_inc(ln_rstd[t], 1)
                pool.wait_ge(ln_rstd[t], seq.times(1))
                pool.tensor_tensor(shift[t][:, :], neg_mean[t][:, :], rstd[t][:, :], ALU.mult).then_inc(ln_shift[t], 1)

            def split(f, i):
                r = f.ring
                left = qk if i == 0 else rest[i - 1]
                if i == 0:
                    pool.wait_ge(qk_done, f.times(2))
                    if f.follows(RING):
                        pool.wait_ge(parts_out[r], f.back(RING).landed(PARTS_DMAS))
                else:
                    pool.wait_ge(split_done, f.times(5, 2 * i))
                hold(pool, pool_passed)
                pool.tensor_scalar(parts[:, r, i], left[:, :, :], 1.0, 0.0, ALU.mult, ALU.add).then_inc(split_done, 1)
                if i < 2:
                    pool.wait_ge(split_done, f.times(5, 2 * i + 1))
                    pool.tensor_tensor(rest[i][:, :, :], left[:, :, :], parts[:, r, i], ALU.subtract).then_inc(split_done, 1)

            def step(ahead, front, maxima, heads, middle, linear, last):
                for slot in range(SLOTS):
                    if front and slot == 0:
                        split(front, 0)
                    if last and slot == 1:
                        norm_scale("f1", last)
                    if front and slot == 1:
                        split(front, 1)
                        split(front, 2)
                    if middle and slot == 2:
                        m = middle
                        pool.wait_ge(x_mid_in[m.ring], m.landed(1))
                        if m.follows(1):
                            pool.wait_ge(x1_done, m.back(1).times(1))
                        pool.tensor_tensor(x_bp[:, 0, :], x_mid[:, m.ring, 0, :], bias_row[:, BP, :], ALU.add)
                        pool.tensor_tensor(x_bp[:, 1, :], x_mid[:, m.ring, 1, :], bias_row[:, BP, :], ALU.add).then_inc(xbp_done, 1)
                    if linear and slot == 5:
                        u = linear
                        pool.wait_ge(x2_done, u.times(1))
                        if u.follows(1):
                            pool.wait_ge(x3_done, u.back(1).times(1))
                        for t in range(TT):
                            ins = pool.tensor_tensor(x2_bc[:, t, :], x2[:, t, :], bias_row[:, BC1, :], ALU.add)
                        ins.then_inc(x2bc_done, 1)
                    if middle and slot == 8:
                        norm_scale("f0", middle)
                    if last and slot in (9, 10):
                        l, c = last, slot - 9
                        pool.wait_ge(hid_done, l.times(2, c + 1))
                        if l.follows(1):
                            pool.wait_ge(proj_mm, l.back(1).times(1))
                        pool.tensor_tensor(hid2[:, 2 * c:2 * c + 2, :], hid[:, 2 * c:2 * c + 2, :], hid[:, 2 * c:2 * c + 2, :],
                                           ALU.mult).then_inc(hid2_done, 1)
                    if ahead and slot == 9:
                        norm_scale("a0", ahead)
                    if middle and slot == 14:
                        norm_scale("a1", middle)

            run_steps(pool, step, {-2: masks, 1: biases})

        @block.scalar
        def _(act):
            def normalise(t, seq, src):
                act.wait_ge(ln_shift[t], seq.times(1))
                if seq.follows(1):
                    act.wait_ge(xn_turned[t], seq.back(1).times(1))
                for i in range(TT):
                    nc.scalar.activation(xn[t][:, i, :], src[:, i, :], ACT.Identity, bias=shift[t][:, i:i + 1],
                                         scale=rstd[t][:, i:i + 1]).then_inc(ln_done[t], 1)

            def copy_turned(t, seq, bank, users):
                act.wait_ge(xn_turned[t], seq.times(1))
                if seq.follows(1):
                    for signal, per in users:
                        act.wait_ge(signal, seq.back(1).times(per))
                nc.scalar.activation(xnT[t][:, :], bank[:, 0:S], ACT.Copy).then_inc(xnT_done[t], 1)

            def exp_head(heads, slot):
                act.wait_ge(score_mm, heads.times(H, slot + 1))
                if heads.follows(1) or slot >= PT_RING:
                    act.wait_ge(pv_mm, heads.times(4, (slot - PT_RING) // 4 + 1))
                nc.scalar.activation(probs[:, slot % PT_RING, :, :].rearrange("p t s -> p (t s)"),
                                     score_bank[slot % 2][:, :], ACT.Exp, scale=SCALE).then_inc(exp_done, 1)

            def step(ahead, front, maxima, heads, middle, linear, last):
                for slot in range(SLOTS):
                    if heads and slot > 0:
                        exp_head(heads, slot)
                    if front and slot == 0:
                        act.wait_ge(qk_mm, front.times(1))
                        if front.follows(1):
                            act.wait_ge(split_done, front.back(1).times(5))
                        for i in range(2):
                            nc.scalar.activation(qk[:, i, :], front_bank[:, i * S:(i + 1) * S], ACT.Identity,
                                                 bias=bias_col[:, i:i + 1]).then_inc(qk_done, 1)
                    if middle and slot == 0:
                        act.wait_ge(pv_mm, middle.times(4))
                        if middle.follows(1):
                            act.wait_ge(yraw_turned, middle.back(1).times(1))
                        nc.scalar.activation(yT_raw[:, :, :].rearrange("p b s -> p (b s)"), pv_bank[:, :], ACT.Copy).then_inc(yraw_done, 1)
                    if heads and slot == 0:
                        exp_head(heads, slot)
                    if linear and slot == 1:
                        copy_turned("a1", linear, mid_bank, ((kv1_mm, 1), (q1_mm, 1)))
                    if last and slot == 3:
                        normalise("f1", last, x3)
                    if linear and slot == 4:
                        act.wait_ge(q1_mm, linear.times(1))
                        if linear.follows(1):
                            act.wait_ge(q1_done, linear.back(1).times(1))
                        nc.scalar.activation(q1[:, :], front_bank[:, 0:S], ACT.Identity, bias=bias_col[:, 2:3]).then_inc(q1_bias, 1)
                        act.wait_ge(k1_min_done, linear.times(1))
                        if linear.follows(1):
                            act.wait_ge(k1_done, linear.back(1).times(1))
                        nc.scalar.activation(k1_exp[:, :, :], k1_min[:, :, :], ACT.Exp).then_inc(k1_exp_done, 1)
                    if middle and slot == 5:
                        act.wait_ge(y0_turned, middle.times(1))
                        if middle.follows(1):
                            act.wait_ge(wp_mm, middle.back(1).times(1))
                        nc.scalar.activation(yT[:, :], mid_bank[:, 0:S], ACT.Copy).then_inc(yT_done, 1)
                    if last and slot == 6:
                        copy_turned("f1", last, last_bank, ((hid_mm, 2),))
                    if linear and slot == 6:
                        act.wait_ge(q1_min_done, linear.times(1))
                        nc.scalar.activation(q1_exp[:, :], q1_min[:, :], ACT.Exp).then_inc(q1_exp_done, 1)
                    if last and slot in (8, 9):
                        c = (slot - 8) // 1
                        act.wait_ge(hid_mm, last.times(2, c + 1))
                        if last.follows(1):
                            act.wait_ge(hid2_done, last.back(1).times(2))
                        nc.scalar.activation(hid[:, 2 * c:2 * c + 2, :].rearrange("p c s -> p (c s)"), (last_bank, mid_bank)[c][:, :],
                                             ACT.Relu).then_inc(hid_done, 1)
                    if middle and slot == 9:
                        normalise("f0", middle, x1)
                    if middle and slot == 11:
                        copy_turned("f0", middle, mid_bank, ((ffn_mm, 1),))
                    if ahead and slot == 11:
                        act.wait_ge(x_in[ahead.ring], ahead.landed(1))
                        normalise("a0", ahead, x_front[:, ahead.ring])
                    if linear and slot == 12:
                        act.wait_ge(y1_turned, linear.times(1))
                        if linear.follows(1):
                            act.wait_ge(wc_mm, linear.back(1).times(1))
                        nc.scalar.activation(y1T[:, :], front_bank[:, 0:S], ACT.Copy).then_inc(y1T_done, 1)
                    if ahead and slot == 14:
                        copy_turned("a0", ahead, front_bank, ((qk_mm, 1), (v_mm, 1)))
                    if middle and slot == 15:
                        normalise("a1", middle, x2)

            run_steps(act, step)

        @block.vector
        def _(dve):
            made = [0]

            def after(ins):
                ins.then_inc(weights_ready, 1)
                made[0] += 1
                dve.wait_ge(weights_ready, made[0])

            nc.vector.memset(v_hat[:, :, :, :, :], 0.0).then_inc(small_made, 1)
            nc.vector.memset(v1_ones[:, :, :], 1.0).then_inc(small_made, 1)
            nc.vector.memset(neg_max[:, :], 0.0).then_inc(small_made, 1)
            dve.wait_ge(small_made, 3)
            for par in range(2):
                vh = v_hat[:, :, :, par::2, 16 * par + DK].rearrange("p r t h -> p (r t) h")
                nc.vector.memset(vh, 1.0).then_inc(small_made, 1)
            dve.wait_ge(small_made, 5)

            def first_weights():
                dve.wait_ge(weight_turned, 1)
                nc.vector.tensor_copy(wT[:, 0:3, :], front_bank[:, 0:3 * P].rearrange("p (a b) -> p a b", a=3)).then_inc(weight_copied, 1)
                nc.vector.memset(k_stack[:, :, :, :].rearrange("p r h s -> p (r h s)").bitcast(F32), 0.0).then_inc(stacks_ready, 1)
                dve.wait_ge(first_in, 16 * FIRST_DMAS)

            def other_weights():
                dve.wait_ge(weights_in, 16 * WEIGHT_DMAS)
                dve.wait_ge(consts_made, 2)
                for c in range(HC + 1):
                    src = raw_fc[:, c, :] if c < HC else raw_proj[:, :]
                    after(nc.vector.tensor_reduce(row_sum[:, c:c + 1], src, AX.X, ALU.add, apply_absolute_value=True))
                after(nc.vector.tensor_scalar(row_scale[:, 0:HC], row_sum[:, 0:HC], 1.0 / D, MIN_SCALE, ALU.mult, ALU.max))
                after(nc.vector.tensor_scalar(row_scale[:, HC:HC + 1], row_sum[:, HC:HC + 1], 1.0 / HID, MIN_SCALE, ALU.mult, ALU.max))
                after(nc.vector.tensor_scalar(half_scale[:, :], row_scale[:, :], 0.5, None, ALU.mult))
                after(nc.vector.tensor_scalar(neg_half[:, :], row_scale[:, :], -0.5, None, ALU.mult))
                for c in range(HC + 1):
                    src = raw_fc[:, c, :] if c < HC else raw_proj[:, :]
                    w = src.shape[-1]
                    after(nc.vector.tensor_scalar(tern_pos[:, 0:w], src, half_scale[:, c:c + 1], row_scale[:, c:c + 1], ALU.is_gt, ALU.mult))
                    after(nc.vector.tensor_scalar(tern_neg[:, 0:w], src, neg_half[:, c:c + 1], row_scale[:, c:c + 1], ALU.is_lt, ALU.mult))
                    after(nc.vector.tensor_tensor(src, tern_pos[:, 0:w], tern_neg[:, 0:w], ALU.subtract))
                ternary_made[0] = made[0]
                dve.wait_ge(weight_turned, 2)
                nc.vector.tensor_copy(wT[:, 3:7, :], mid_bank[:, :].rearrange("p (a b) -> p a b", a=4)).then_inc(weight_copied, 1)
                dve.wait_ge(weight_turned, 3)
                nc.vector.tensor_copy(wT[:, 7:9, :], last_bank[:, 0:2 * P].rearrange("p (a b) -> p a b", a=2)).then_inc(weight_copied, 1)
                nc.vector.tensor_copy(fbT[:, :], last_bank[:, 2 * P:3 * P]).then_inc(weight_copied, 1)
                dve.wait_ge(weight_turned, 4)
                nc.vector.tensor_copy(uT[:, :], mid_bank[:, :]).then_inc(weight_copied, 1)
                dve.wait_ge(weight_turned, 5)
                nc.vector.tensor_copy(fcT[:, :], last_bank[:, :]).then_inc(weight_copied, 1)
                dve.wait_ge(weight_turned, 6)
                nc.vector.tensor_copy(projT[:, :, :], mid_bank[:, :].rearrange("p (a b) -> p a b", a=HC)).then_inc(weight_copied, 1)

            def pooled_term():
                dve.wait_ge(weight_copied, 7)
                after(nc.vector.tensor_tensor(wT[:, WF, :], wT[:, WF, :], disha2[:, :], ALU.add))
                dve.wait_ge(weight_turned, 7)
                after(nc.vector.tensor_scalar(fbv[:, :], last_bank[0:RK, 0:P], gate_col[:, 0:1], None, ALU.mult))
                fbv_made[0] = made[0]

            def low_rank_term():
                dve.wait_ge(weight_turned, 8)
                after(nc.vector.tensor_tensor(fcT[:, :], last_bank[:, :], fcT[:, :], ALU.add))
                all_made[0] = made[0]

            def norm_stats(t, seq, src):
                if seq.follows(1):
                    dve.wait_ge(ln_mv[t], seq.back(1).times(2))
                for i in range(TT):
                    nc.vector.bn_stats(stats[t][:, i, :], src[:, i, :]).then_inc(ln_stats[t], 1)
                dve.wait_ge(ln_stats[t], seq.times(2))
                if seq.follows(1):
                    dve.wait_ge(ln_pre[t], seq.back(1).times(2))
                hold(dve, dve_passed)
                for i in range(TT):
                    nc.vector.bn_aggr(mv[t][:, i, :], stats[t][:, i, :]).then_inc(ln_mv[t], 1)

            def tile3(ap, b):
                return ap.rearrange("p (t d) -> p t d", t=b)

            def reduce_tile(a, tile):
                t, j = tile // PAIRS, tile % PAIRS
                dve.wait_ge(max_mm, a.times(16, tile + 1))
                if tile == 0 and a.follows(1):
                    dve.wait_ge(max_turned, a.back(1).times(1))
                dst = neg_max[:, 0:32].rearrange("p (h j t) -> p h j t", h=2, t=TT)[:, :, j, t]
                nc.vector.tensor_reduce(dst, tile3(max_bank[tile % 2][:, :], 2), AX.X, ALU.max,
                                        negate=True).then_inc(max_done, 1)

            def step(ahead, front, maxima, heads, middle, linear, last):
                for slot in range(SLOTS):
                    if last and slot == 0:
                        l = last
                        dve.wait_ge(wc_mm, l.times(1))
                        dve.wait_ge(x2bc_done, l.times(1))
                        if l.follows(1):
                            dve.wait_ge(x4_done, l.back(1).times(1))
                            dve.wait_ge(ln_done["f1"], l.back(1).times(2))
                        nc.vector.tensor_tensor(x3[:, :, :], tile3(last_bank[:, 0:S], TT), x2_bc[:, :, :], ALU.add).then_inc(x3_done, 1)
                        dve.wait_ge(x3_done, l.times(1))
                        norm_stats("f1", l, x3)
                    if maxima and MAX_TILES[slot] >= 1:
                        reduce_tile(maxima, sum(MAX_TILES[:slot]))
                    if maxima and slot == 13:
                        a = maxima
                        dve.wait_ge(max_turned, a.times(1))
                        if a.follows(1):
                            dve.wait_ge(aug_in[a.back(1).ring], a.back(1).landed(AUG_DMAS))
                        nc.vector.tensor_copy(neg_max_parts[:, 0, :], max_bank[1][0:32, 0:P]).then_inc(max_parts, 1)
                        dve.wait_ge(max_parts, a.times(2, 1))
                        nc.vector.tensor_tensor(neg_max_parts[:, 1, :], max_bank[1][0:32, 0:P], neg_max_parts[:, 0, :],
                                                ALU.subtract).then_inc(max_parts, 1)
                    if front and slot == 2:
                        f = front
                        dve.wait_ge(v_mm, f.times(1))
                        if f.follows(RING):
                            dve.wait_ge(pv_mm, f.back(RING).times(4))
                        for par in range(2):
                            dst = v_hat[:, f.ring, :, par::2, 16 * par:16 * par + DK]
                            src = front_bank[:, 0:S].rearrange("p (t h a d) -> p t h a d", t=TT, a=2, d=DK)[:, :, :, par, :]
                            b = bias_row[:, BV:BV + 1, :].rearrange("p o (h a d) -> p o h a d", a=2, d=DK)[:, :, :, par, :]
                            nc.vector.tensor_tensor(dst, src, b.broadcast_to([P, TT, PAIRS, DK]), ALU.add).then_inc(v_done, 1)
                    if middle and slot == 3:
                        m = middle
                        dve.wait_ge(yraw_turned, m.times(1))
                        if m.follows(1):
                            dve.wait_ge(y0_turned, m.back(1).times(1))
                        heads_view = mid_bank[:, :].rearrange("p (n c) -> p n c", c=16)
                        nc.vector.reciprocal(inv_den[:, :], heads_view[:, :, DK]).then_inc(den_done, 1)
                        dve.wait_ge(den_done, m.times(1))
                        nc.vector.tensor_tensor(y0[:, :, :], heads_view[:, :, 0:DK],
                                                inv_den[:, :].unsqueeze(2).broadcast_to([P, TT * H, DK]), ALU.mult).then_inc(y0_done, 1)
                    if linear:
                        u = linear
                        if slot == 3:
                            dve.wait_ge(kv1_mm, u.times(1))
                            if u.follows(1):
                                dve.wait_ge(k1_done, u.back(1).times(1))
                                dve.wait_ge(state_mm, u.back(1).times(1))
                            kv = tile3(last_bank[:, :], TT)
                            nc.vector.tensor_tensor(k1[:, :, :], kv[:, :, 0:P], bias_row[:, BK1:BK1 + 1, :].broadcast_to([P, TT, P]), ALU.add).then_inc(kv1_bias, 1)
                            nc.vector.tensor_tensor(v1_ones[:, :, 0:P], kv[:, :, P:2 * P], bias_row[:, BV1:BV1 + 1, :].broadcast_to([P, TT, P]), ALU.add).then_inc(kv1_bias, 1)
                            dve.wait_ge(kv1_bias, u.times(2, 1))
                            if u.follows(1):
                                dve.wait_ge(k1_exp_done, u.back(1).times(1))
                            nc.vector.tensor_scalar(k1_min[:, :, :], k1[:, :, :], 0.0, None, ALU.min).then_inc(k1_min_done, 1)
                        if slot == 5:
                            dve.wait_ge(k1_exp_done, u.times(1))
                            if u.follows(1):
                                dve.wait_ge(state_mm, u.back(1).times(1))
                            nc.vector.scalar_tensor_tensor(k1_elu[:, :, :], k1[:, :, :], 0.0, k1_exp[:, :, :], ALU.max, ALU.add).then_inc(k1_done, 1)
                            dve.wait_ge(q1_bias, u.times(1))
                            if u.follows(1):
                                dve.wait_ge(q1_exp_done, u.back(1).times(1))
                            nc.vector.tensor_scalar(q1_min[:, :], q1[:, :], 0.0, None, ALU.min).then_inc(q1_min_done, 1)
                        if slot == 7:
                            dve.wait_ge(state_mm, u.times(1))
                            if u.follows(1):
                                dve.wait_ge(y1_mm, u.back(1).times(1))
                            nc.vector.tensor_tensor(kv_blocks[:, 0:P], front_bank[:, 0:P], block_mask[:, :], ALU.mult).then_inc(state_done, 1)
                            nc.vector.tensor_scalar(kv_blocks[:, P:P + H], head_mask[:, :], front_bank[:, P:P + 1], None, ALU.mult).then_inc(state_done, 1)
                            dve.wait_ge(q1_exp_done, u.times(1))
                            nc.vector.scalar_tensor_tensor(q1_elu[:, :], q1[:, :], 0.0, q1_exp[:, :], ALU.max, ALU.add).then_inc(q1_done, 1)
                        if slot == 9:
                            dve.wait_ge(y1_mm, u.times(1))
                            if u.follows(1):
                                dve.wait_ge(y1_done, u.back(1).times(1))
                            y1p = tile3(front_bank[:, 0:TT * (P + H)], TT)
                            nc.vector.tensor_scalar(den1[:, :, :], y1p[:, :, P:P + H], Z_EPS, None, ALU.add).then_inc(den1_done, 1)
                            dve.wait_ge(den1_done, u.times(2, 1))
                            nc.vector.reciprocal(inv_den1[:, :, :], den1[:, :, :]).then_inc(den1_done, 1)
                            dve.wait_ge(den1_done, u.times(2, 2))
                            if u.follows(1):
                                dve.wait_ge(y1_turned, u.back(1).times(1))
                            for t in range(TT):
                                ins = nc.vector.tensor_tensor(y1[:, t], y1p[:, t, 0:P].rearrange("p (h d) -> p h d", d=DK),
                                                              inv_den1[:, t, :].unsqueeze(2).broadcast_to([P, H, DK]), ALU.mult)
                            ins.then_inc(y1_done, 1)
                    if middle:
                        m = middle
                        if slot == 7:
                            dve.wait_ge(wp_mm, m.times(1))
                            dve.wait_ge(xbp_done, m.times(1))
                            if m.follows(1):
                                dve.wait_ge(x2_done, m.back(1).times(1))
                                dve.wait_ge(ln_done["f0"], m.back(1).times(2))
                            nc.vector.tensor_tensor(x1[:, :, :], tile3(mid_bank[:, 0:S], TT), x_bp[:, :, :], ALU.add).then_inc(x1_done, 1)
                            dve.wait_ge(x1_done, m.times(1))
                            norm_stats("f0", m, x1)
                        if slot == 13:
                            dve.wait_ge(ffn_mm, m.times(1))
                            if m.follows(1):
                                dve.wait_ge(ln_done["a1"], m.back(1).times(2))
                                dve.wait_ge(x2bc_done, m.back(1).times(1))
                            nc.vector.tensor_tensor(x2[:, :, :], tile3(mid_bank[:, 0:S], TT), x1[:, :, :], ALU.add).then_inc(x2_done, 1)
                            dve.wait_ge(x2_done, m.times(1))
                            norm_stats("a1", m, x2)
                    if ahead and slot == 8:
                        dve.wait_ge(x_in[ahead.ring], ahead.landed(1))
                        norm_stats("a0", ahead, x_front[:, ahead.ring])
                    if last and slot == 14:
                        l = last
                        dve.wait_ge(proj_mm, l.times(1))
                        if l.follows(1):
                            dve.wait_ge(out_done[l.back(1).ring], l.back(1).landed(1))
                        nc.vector.tensor_tensor(x4[:, :, :], tile3(last_bank[:, 0:S], TT), x3[:, :, :], ALU.add).then_inc(x4_done, 1)
                    if maxima and MAX_TILES[slot] == 2:
                        reduce_tile(maxima, sum(MAX_TILES[:slot]) + 1)

            run_steps(dve, step, {-2: first_weights, -1: other_weights, 0: pooled_term, 1: low_rank_term})

        @block.tensor
        def _(pe):
            def turn_all(bank, srcs):
                for i, s in enumerate(srcs):
                    ins = nc.tensor.transpose(bank[:, i * P:(i + 1) * P], s, ident[:, :])
                ins.then_inc(weight_turned, 1)

            def first_weights():
                pe.wait_ge(ident_made, 1)
                pe.wait_ge(first_in, 16 * FIRST_DMAS)
                turn_all(front_bank, [raw[:, i, :] for i in (WQ, WK, WV)])
                pe.wait_ge(weight_copied, 1)

            def other_weights():
                pe.wait_ge(weights_in, 16 * WEIGHT_DMAS)
                turn_all(mid_bank, [raw[:, i, :] for i in range(3, 7)])
                turn_all(last_bank, [raw[:, 7, :], raw[:, 8, :], raw_fb[:, :]])
                pe.wait_ge(weight_copied, 2)
                turn_all(mid_bank, [raw_u[:, c, :] for c in range(HC)])
                pe.wait_ge(weight_copied, 4)
                pe.wait_ge(weights_ready, ternary_made[0])
                turn_all(last_bank, [raw_fc[:, c, :] for c in range(HC)])
                pe.wait_ge(weight_copied, 5)
                turn_all(mid_bank, [raw_proj[:, c * P:(c + 1) * P] for c in range(HC)])
                pe.wait_ge(ones_in, 32)

            def low_rank():
                pe.wait_ge(weight_copied, 7)
                nc.tensor.matmul(last_bank[0:RK, 0:P], fbT[0:RK, 0:RK], raw_v[:, :], start=True, stop=True).then_inc(weight_turned, 1)

            def low_rank_term():
                pe.wait_ge(weights_ready, fbv_made[0])
                nc.tensor.matmul(last_bank[:, :], fbv[:, :], uT[0:RK, :], start=True, stop=True).then_inc(weight_turned, 1)

            def all_weights():
                pe.wait_ge(weights_ready, all_made[0])

            def turn_tokens(bank, src, signal):
                for t in range(TT):
                    ins = nc.tensor.transpose(bank[:, t * P:(t + 1) * P], src(t), ident[:, :])
                ins.then_inc(signal, 1)

            def by_token(bank, lhs, w, signal, width=P):
                for t in range(TT):
                    ins = nc.tensor.matmul(bank[:, t * width:(t + 1) * width], lhs[:, t * P:(t + 1) * P], w, start=True, stop=True)
                ins.then_inc(signal, 1)

            def pv(heads, g):
                v, b, a = heads.ring, g // 2, g % 2
                pe.wait_ge(exp_done, heads.times(H, 4 * g + 4))
                if g == 0 and heads.follows(1):
                    pe.wait_ge(yraw_done, heads.back(1).times(1))
                for t in range(TT):
                    for j in range(4):
                        h = 8 * b + 2 * j + a
                        ins = nc.tensor.matmul(pv_bank[32 * j:32 * j + 32, b * S:(b + 1) * S], v_hat[:, v, t, h, :],
                                               probs[:, (4 * g + j) % PT_RING, t, :], start=(a == 0 and t == 0),
                                               stop=(a == 1 and t == TT - 1))
                ins.then_inc(pv_mm, 1)

            def project(l, t):
                for c in range(HC):
                    ins = nc.tensor.matmul(last_bank[:, t * P:(t + 1) * P], hid2[:, c, t * P:(t + 1) * P],
                                           projT[:, c, :], start=(c == 0), stop=(c == HC - 1))
                return ins

            def head_scores(heads, slot):
                r = heads.ring
                h = 8 * (slot // 8) + 2 * (slot % 4) + slot // 4 % 2
                if slot == 0:
                    pe.wait_ge(aug_in[r], heads.landed(AUG_DMAS))
                if heads.follows(1) or slot >= 2:
                    pe.wait_ge(exp_done, heads.times(H, slot - 1))
                for t in range(TT):
                    ins = nc.tensor.matmul(score_bank[slot % 2][:, t * S:(t + 1) * S], k_stack[:, r, h, t * P:(t + 1) * P],
                                           q_stack[:, r, h // 2, :], start=True, stop=True)
                ins.then_inc(score_mm, 1)

            def max_tile(a, tile):
                t, j, r = tile // PAIRS, tile % PAIRS, a.ring
                if tile == 0:
                    pe.wait_ge(stack_in[r], a.landed(STACK_DMAS))
                if tile == 1 and a.follows(1):
                    pe.wait_ge(max_parts, a.back(1).times(2))
                if tile >= 2:
                    pe.wait_ge(max_done, a.times(16, tile - 1))
                nc.tensor.matmul(max_bank[tile % 2][:, :], q_stack[:, r, j, t * P:(t + 1) * P],
                                 k_stack[:, r, 2 * j:2 * j + 2, :].rearrange("p h s -> p (h s)"), start=True, stop=True).then_inc(max_mm, 1)

            def step(ahead, front, maxima, heads, middle, linear, last):
                for slot in range(SLOTS):
                    if heads and slot > 0:
                        head_scores(heads, slot)
                    if maxima and MAX_TILES[slot] >= 1:
                        max_tile(maxima, sum(MAX_TILES[:slot]))
                    if heads and slot in (5, 10, 14):
                        pv(heads, (slot - 5) // 4)
                    if middle and slot == 0:
                        pv(middle, 3)
                    if linear and slot == 0:
                        pe.wait_ge(ln_done["a1"], linear.times(2))
                        turn_tokens(mid_bank, lambda t: xn["a1"][:, t, :], xn_turned["a1"])
                    if heads and slot == 0:
                        head_scores(heads, slot)
                    if front and slot == 1:
                        pe.wait_ge(qk_done, front.times(2))
                        by_token(front_bank, xnT["a0"], wT[:, WV, :], v_mm)
                    if middle:
                        m = middle
                        if slot == 2:
                            pe.wait_ge(yraw_done, m.times(1))
                            if linear:
                                pe.wait_ge(xnT_done["a1"], linear.times(1))
                            for t in range(TT):
                                for b in range(2):
                                    ins = nc.tensor.transpose(mid_bank[:, (2 * t + b) * P:(2 * t + b + 1) * P],
                                                              yT_raw[:, b, t * P:(t + 1) * P], ident[:, :])
                            ins.then_inc(yraw_turned, 1)
                        if slot == 4:
                            pe.wait_ge(y0_done, m.times(1))
                            turn_tokens(mid_bank, lambda t: y0[:, t * H:(t + 1) * H, :].rearrange("p h d -> p (h d)"), y0_turned)
                        if slot == 11:
                            pe.wait_ge(ln_done["f0"], m.times(2))
                            if last:
                                pe.wait_ge(hid_done, last.times(2))
                            turn_tokens(mid_bank, lambda t: xn["f0"][:, t, :], xn_turned["f0"])
                        if slot == 12:
                            pe.wait_ge(xnT_done["f0"], m.times(1))
                            by_token(mid_bank, xnT["f0"], wT[:, WF, :], ffn_mm)
                    if linear:
                        u = linear
                        if slot == 2:
                            pe.wait_ge(xnT_done["a1"], u.times(1))
                            if last:
                                pe.wait_ge(x3_done, last.times(1))
                            by_token(last_bank, xnT["a1"], wT[:, WK1:WV1 + 1, :].rearrange("p a b -> p (a b)"), kv1_mm, 2 * P)
                        if slot == 3:
                            if front:
                                pe.wait_ge(v_done, front.times(2))
                            elif u.follows(1):
                                pe.wait_ge(y1T_done, u.back(1).times(1))
                            nc.tensor.matmul(front_bank[:, 0:S], wT[:, WQ1, :], xnT["a1"][:, :], start=True, stop=True).then_inc(q1_mm, 1)
                        if slot == 6:
                            pe.wait_ge(k1_done, u.times(1))
                            pe.wait_ge(q1_bias, u.times(1))
                            for t in range(TT):
                                ins = nc.tensor.matmul(front_bank[:, 0:P + 1], k1_elu[:, t, :], v1_ones[:, t, :], start=(t == 0), stop=(t == TT - 1))
                            ins.then_inc(state_mm, 1)
                        if slot == 11:
                            pe.wait_ge(y1_done, u.times(1))
                            turn_tokens(front_bank, lambda t: y1[:, t].rearrange("p h d -> p (h d)"), y1_turned)
                        if slot == 15:
                            pe.wait_ge(y1T_done, u.times(1))
                            if last:
                                pe.wait_ge(x4_done, last.times(1))
                            by_token(last_bank, y1T, wT[:, WC1, :], wc_mm)
                    if middle and slot == 6:
                        pe.wait_ge(yT_done, middle.times(1))
                        by_token(mid_bank, yT, wT[:, WP_, :], wp_mm)
                    if last:
                        l = last
                        if slot == 5:
                            pe.wait_ge(ln_done["f1"], l.times(2))
                            if linear:
                                pe.wait_ge(kv1_bias, linear.times(2))
                            turn_tokens(last_bank, lambda t: xn["f1"][:, t, :], xn_turned["f1"])
                        if slot in (7, 8):
                            half = slot - 7
                            pe.wait_ge(xnT_done["f1"], l.times(1))
                            if half == 1 and middle:
                                pe.wait_ge(x1_done, middle.times(1))
                            for i in range(2):
                                c = 2 * half + i
                                ins = nc.tensor.matmul((last_bank, mid_bank)[half][:, i * S:(i + 1) * S], fcT[:, c * P:(c + 1) * P], xnT["f1"][:, :],
                                                       start=True, stop=True)
                            ins.then_inc(hid_mm, 1)
                        if slot == 12:
                            pe.wait_ge(hid_done, l.times(2))
                            pe.wait_ge(hid2_done, l.times(2))
                            project(l, 0)
                        if slot == 13:
                            project(l, 1).then_inc(proj_mm, 1)
                    if linear and slot == 8:
                        pe.wait_ge(state_done, linear.times(2))
                        pe.wait_ge(q1_done, linear.times(1))
                        by_token(front_bank, q1_elu, kv_blocks[:, :], y1_mm, P + H)
                    if ahead:
                        a = ahead
                        if slot == 13:
                            pe.wait_ge(ln_done["a0"], a.times(2))
                            if linear:
                                pe.wait_ge(y1T_done, linear.times(1))
                            elif a.follows(1):
                                pe.wait_ge(v_done, a.back(1).times(2))
                            turn_tokens(front_bank, lambda t: xn["a0"][:, t, :], xn_turned["a0"])
                        if slot == 15:
                            pe.wait_ge(xnT_done["a0"], a.times(1))
                            for i, w in enumerate((WQ, WK)):
                                ins = nc.tensor.matmul(front_bank[:, i * S:(i + 1) * S], wT[:, w, :], xnT["a0"][:, :], start=True, stop=True)
                            ins.then_inc(qk_mm, 1)
                    if maxima and MAX_TILES[slot] == 2:
                        max_tile(maxima, sum(MAX_TILES[:slot]) + 1)
                    if maxima and slot == 12:
                        pe.wait_ge(max_done, maxima.times(16))
                        nc.tensor.transpose(max_bank[1][:, 0:P], neg_max[:, :], ident[:, :]).then_inc(max_turned, 1)

            run_steps(pe, step, {-3: first_weights, -1: other_weights, 0: low_rank, 1: low_rank_term, 2: all_weights})


_INS = ['L0_attn_x', 'L0_attn_Wq', 'L0_attn_bq', 'L0_attn_Wk', 'L0_attn_bk', 'L0_attn_Wv', 'L0_attn_bv',
        'L0_attn_Wp', 'L0_attn_bp', 'L0_ffn_weight', 'L0_ffn_disha', 'L1_attn_Wq', 'L1_attn_bq', 'L1_attn_Wk',
        'L1_attn_bk', 'L1_attn_Wv', 'L1_attn_bv', 'L1_attn_Wc', 'L1_attn_bc', 'L1_ffn_fast_b', 'L1_ffn_w_fc',
        'L1_ffn_w_proj', 'L1_ffn_u', 'L1_ffn_v', 'L1_ffn_gate']


def kernel(**inputs):
    import numpy as _np
    import concourse.bacc as _bacc
    from concourse import mybir as _mybir
    from concourse.bass_utils import run_bass_kernel_spmd as _run

    nc = _bacc.Bacc("TRN2", target_bir_lowering=False, num_devices=1)
    arrays, args = {}, []
    for name in _INS:
        a = _np.ascontiguousarray(inputs[name])
        if a.ndim == 0:
            a = a.reshape(1)
        arrays[f"in_{name}_dram"] = a
        args.append(nc.dram_tensor(f"in_{name}_dram", a.shape, _mybir.dt.from_np(a.dtype), kind="ExternalInput").ap())
    shape = arrays["in_L0_attn_x_dram"].shape
    args.append(nc.dram_tensor("out_0_dram", shape, _mybir.dt.float32, kind="ExternalOutput").ap())
    two_layer_kernel(nc, *args)
    r = _run(nc, [arrays], core_ids=[0])
    return r.results[0]["out_0_dram"]
```
